# Optimizing a Trainium2 kernel written in Bass

```python
import numpy as np
import jax
import jax.numpy as jnp

def _softmax(x, axis=-1):
    return jax.nn.softmax(x, axis=axis)

def _gelu(x):
    return jax.nn.gelu(x, approximate=True)

def _silu(x):
    return jax.nn.silu(x)

def _sigmoid(x):
    return jax.nn.sigmoid(x)

def _layernorm(x, axis=-1, eps=1e-05):
    m = jnp.mean(x, axis=axis, keepdims=True)
    v = jnp.var(x, axis=axis, keepdims=True)
    return (x - m) / jnp.sqrt(v + eps)

def _scatter_add(tgt, idx, src, axis=0):
    return tgt.at[idx].add(src)

def _segment_sum(src, seg, n):
    return jax.ops.segment_sum(src, seg, n)
kernel_name = 'mk_adj_resnorm_d2_adj_r2_ce3412'

def setup_inputs(seed: int=0):
    np.random.seed(seed)
    _w = jnp.asarray

    def _rec_inputs():
        import jax
        import jax.numpy as jnp
        _gk = jax.random.key(seed)
        x = -0.000125 + 0.9999 * jax.random.normal(jax.random.fold_in(_gk, 1), (32, 256, 128), jnp.float32)
        _w = (1.0 + jnp.arange(256, dtype=jnp.float32)) ** (-0.5)
        _w = _w / _w.mean()
        _pij = jnp.clip(0.0078125 * _w[:, None] * _w[None, :], 0.0, 1.0)
        _a = jax.random.uniform(jax.random.fold_in(_gk, 2), (256, 256)) < _pij
        _a = jnp.logical_or(_a, jnp.swapaxes(_a, -1, -2))
        _a = jnp.logical_or(_a, jnp.eye(256, dtype=bool))
        _af = _a.astype(jnp.float32)
        _af = _af * jax.random.uniform(jax.random.fold_in(_gk, 3), (256, 256), jnp.float32, 0.05, 0.000488281)
        adj = _af
        return (x, adj)
    x, adj = _rec_inputs()

    def _L0_gnn_setup():
        import jax, jax.numpy as jnp
        import numpy as np
        B, T, D, H = (64, 1024, 128, 128)
        MAX_SKIP = 4

        def _lstm_last(Wih, Whh, bih, bhh, xs):
            N, _, Hd = xs.shape
            bias = bih + bhh

            def step(carry, x_t):
                h, c = carry
                g = x_t @ Wih.T + h @ Whh.T + bias
                i, f, gg, o = jnp.split(g, 4, axis=-1)
                c = jax.nn.sigmoid(f) * c + jax.nn.sigmoid(i) * jnp.tanh(gg)
                h = jax.nn.sigmoid(o) * jnp.tanh(c)
                return ((h, c), None)
            init = (jnp.zeros((N, Hd), xs.dtype), jnp.zeros((N, Hd), xs.dtype))
            (h_last, _), _ = jax.lax.scan(step, init, jnp.swapaxes(xs, 0, 1))
            return h_last
        key = jax.random.key(seed)
        ks = jax.random.split(key, 8)
        s = 0.05
        x = jax.random.normal(ks[0], (B, T, D), jnp.float32)
        adj = jax.random.uniform(ks[1], (T, T), jnp.float32) / T
        Wg0 = jax.random.normal(ks[2], (D, H), jnp.float32) * s
        bg0 = jnp.zeros((H,), jnp.float32)
        Wg1 = jax.random.normal(ks[3], (H, H), jnp.float32) * s
        bg1 = jnp.zeros((H,), jnp.float32)
        Wih = jax.random.normal(ks[4], (MAX_SKIP, 4 * H, H), jnp.float32) * s
        Whh = jax.random.normal(ks[5], (MAX_SKIP, 4 * H, H), jnp.float32) * s
        bih = jax.random.normal(ks[6], (MAX_SKIP, 4 * H), jnp.float32) * s
        bhh = jax.random.normal(ks[7], (MAX_SKIP, 4 * H), jnp.float32) * s
        return dict(x=x, adj=adj, Wg0=Wg0, bg0=bg0, Wg1=Wg1, bg1=bg1, Wih=Wih, Whh=Whh, bih=bih, bhh=bhh)
    _L0_gnn_all = _L0_gnn_setup()
    _L0_gnn_in = {k: v for k, v in _L0_gnn_all.items() if k in ('Wg0', 'bg0', 'Wg1', 'bg1', 'Wih', 'Whh', 'bih', 'bhh')}
    del _L0_gnn_all

    def _L1_gnn_setup():
        import jax, jax.numpy as jnp
        import numpy as np
        B, N, IN_DIM, OUT_DIM, H = (2, 2048, 128, 128, 4)
        HEAD_DIM = OUT_DIM // H
        EDGE_P = 0.01
        key = jax.random.key(seed)
        k1, k2, k3 = jax.random.split(key, 3)
        h = jax.random.normal(k1, (B, N, IN_DIM), dtype=jnp.float32)
        W = jax.random.normal(k2, (IN_DIM, 3 * OUT_DIM), dtype=jnp.float32) / np.sqrt(IN_DIM)
        adj = (jax.random.uniform(k3, (N, N)) < EDGE_P).astype(jnp.float32)
        adj = jnp.maximum(adj, jnp.eye(N, dtype=jnp.float32))
        return {'h': h, 'W': W, 'adj': adj}
    _L1_gnn_all = _L1_gnn_setup()
    _L1_gnn_in = {k: v for k, v in _L1_gnn_all.items() if k in ('W',)}
    del _L1_gnn_all
    return {'x': x, 'adj': adj, 'L0_gnn_Wg0': _L0_gnn_in['Wg0'], 'L0_gnn_bg0': _L0_gnn_in['bg0'], 'L0_gnn_Wg1': _L0_gnn_in['Wg1'], 'L0_gnn_bg1': _L0_gnn_in['bg1'], 'L0_gnn_Wih': _L0_gnn_in['Wih'], 'L0_gnn_Whh': _L0_gnn_in['Whh'], 'L0_gnn_bih': _L0_gnn_in['bih'], 'L0_gnn_bhh': _L0_gnn_in['bhh'], 'L1_gnn_W': _L1_gnn_in['W']}

def reference(x, adj, L0_gnn_Wg0, L0_gnn_bg0, L0_gnn_Wg1, L0_gnn_bg1, L0_gnn_Wih, L0_gnn_Whh, L0_gnn_bih, L0_gnn_bhh, L1_gnn_W):
    import jax
    import jax.numpy as jnp

    def _L0_gnn_ref(x, adj, Wg0, bg0, Wg1, bg1, Wih, Whh, bih, bhh):
        import jax, jax.numpy as jnp
        import numpy as np
        B, T, D, H = (64, 1024, 128, 128)
        MAX_SKIP = 4

        def _lstm_last(Wih, Whh, bih, bhh, xs):
            N, _, Hd = xs.shape
            bias = bih + bhh

            def step(carry, x_t):
                h, c = carry
                g = x_t @ Wih.T + h @ Whh.T + bias
                i, f, gg, o = jnp.split(g, 4, axis=-1)
                c = jax.nn.sigmoid(f) * c + jax.nn.sigmoid(i) * jnp.tanh(gg)
                h = jax.nn.sigmoid(o) * jnp.tanh(c)
                return ((h, c), None)
            init = (jnp.zeros((N, Hd), xs.dtype), jnp.zeros((N, Hd), xs.dtype))
            (h_last, _), _ = jax.lax.scan(step, init, jnp.swapaxes(xs, 0, 1))
            return h_last
        h = jax.nn.relu(jnp.einsum('ts,bsh->bth', adj, x @ Wg0 + bg0))
        h = jax.nn.relu(jnp.einsum('ts,bsh->bth', adj, h @ Wg1 + bg1))
        Bv, Tv, Hd = h.shape
        for p in range(1, MAX_SKIP + 1):
            nw = Tv // p
            wins = h[:, :nw * p, :].reshape(Bv * nw, p, Hd)
            last = _lstm_last(Wih[p - 1], Whh[p - 1], bih[p - 1], bhh[p - 1], wins)
            idx = jnp.arange(nw) * p + (p - 1)
            h = h.at[:, idx, :].set(last.reshape(Bv, nw, Hd))
        return h

    def _L1_gnn_ref(h, W, adj):
        import jax, jax.numpy as jnp
        import numpy as np
        B, N, IN_DIM, OUT_DIM, H = (2, 2048, 128, 128, 4)
        HEAD_DIM = OUT_DIM // H
        EDGE_P = 0.01
        Bn, Nn, _ = h.shape
        qkv = h @ W
        qkv = qkv.reshape(Bn, Nn, 3, H, HEAD_DIM).transpose(2, 0, 3, 1, 4)
        q, k, v = (qkv[0], qkv[1], qkv[2])
        mask = jnp.where(adj == 0, -jnp.inf, 0.0)
        scores = jnp.einsum('bhid,bhjd->bhij', q, k) / np.sqrt(HEAD_DIM) + mask
        attn = jax.nn.softmax(scores, axis=-1)
        out = jnp.einsum('bhij,bhjd->bhid', attn, v)
        return out.transpose(0, 2, 1, 3).reshape(Bn, Nn, OUT_DIM)
    x = _layernorm(x + _L0_gnn_ref(x, adj, L0_gnn_Wg0, L0_gnn_bg0, L0_gnn_Wg1, L0_gnn_bg1, L0_gnn_Wih, L0_gnn_Whh, L0_gnn_bih, L0_gnn_bhh), axis=-1)
    x = _layernorm(x + _L1_gnn_ref(x, L1_gnn_W, adj), axis=-1)
    return x

_drawn_inputs = setup_inputs


def setup_inputs(seed=0):
    import zlib

    import numpy as np

    out = dict(_drawn_inputs(seed))
    spreads = {'L0_gnn_bg0': (0.0, 0.8), 'L0_gnn_bg1': (0.0, 0.8)}
    factors = {'L0_gnn_Wg0': 8.0, 'L0_gnn_Wg1': 8.0, 'L0_gnn_Wih': 8.0, 'L0_gnn_Whh': 8.0}
    for name, (base, spread) in spreads.items():
        noise = np.random.default_rng([zlib.crc32(name.encode()), seed]).standard_normal(out[name].shape)
        drawn = base * np.exp(spread * noise) if base else spread * noise
        out[name] = jnp.asarray(drawn.astype(out[name].dtype))
    for name, factor in factors.items():
        out[name] = (out[name] * factor).astype(out[name].dtype)
    return out
```

```python
from contextlib import ExitStack

import concourse.bass as bass
from concourse import mybir
from concourse.alu_op_type import AluOpType as ALU

F32 = mybir.dt.float32
F32R = mybir.dt.float32r
BF16 = mybir.dt.bfloat16
ACT = mybir.ActivationFunctionType
AX = mybir.AxisListType

P = 128
MASKED = -1.0e30
EPS = 1e-05


def wait(eng, sem, value):
    if isinstance(value, int) and value <= 0:
        return
    eng.wait_ge(sem, value)


def graph_kernel(nc, x, adj, Wg0, bg0, Wg1, bg1, Wih, Whh, bih, bhh, Wqkv, out):
    B, T, D = x.shape
    SKIPS, G4, _ = Wih.shape
    GATES = G4 // P
    TOK = B * T
    UNIT = 512
    UNITS = TOK // UNIT
    BU = UNIT // T
    C = T // P
    CH = TOK // P
    HEADS = 4
    HD = D // HEADS
    SCALE = float(HD) ** -0.5
    assert D == P and T == 256 and GATES == 4 and SKIPS == 4

    x_v = x.rearrange("b (c p) d -> p (b c) d", p=P)
    out_v = out.rearrange("b (c p) d -> p (b c) d", p=P)

    with ExitStack() as top:
        def sb(name, shape, dt, ctx=top):
            return ctx.enter_context(nc.sbuf_tensor(name, shape, dt))

        def sem(name, ctx=top):
            return ctx.enter_context(nc.semaphore(name))

        res = sb("res", [P, CH, D], F32)
        h_hi = sb("h_hi", [P, TOK], F32R)
        h_lo = sb("h_lo", [P, TOK], F32R)
        ident = sb("ident", [P, P], F32)
        ident_bf = sb("ident_bf", [P, P], BF16)
        adj_nat = sb("adj_nat", [P, C, T], F32)
        mask = sb("mask", [P, C, T], BF16)
        wqkv = sb("wqkv", [P, 3 * D], F32)
        head_rows = sb("head_rows", [P, HEADS], F32)

        x_loaded = [sem(f"x_loaded{k}") for k in range(4)]
        ident_made = sem("ident_made")
        ident_bf_made = sem("ident_bf_made")
        rows_made = sem("rows_made")
        mask_made = sem("mask_made")
        adj_loaded = sem("adj_loaded")
        wqkv_loaded = sem("wqkv_loaded")

        with ExitStack() as st:
            w_hi = sb("w_hi", [P, SKIPS, 2, G4], F32R, st)
            w_lo = sb("w_lo", [P, SKIPS, 2, G4], F32R, st)
            adjT_hi = sb("adjT_hi", [P, C, T], F32R, st)
            adjT_lo = sb("adjT_lo", [P, C, T], F32R, st)
            adjT = sb("adjT", [P, C, T], F32, st)
            wg0 = sb("wg0", [P, D], F32, st)
            wg0_hi = sb("wg0_hi", [P, D], F32R, st)
            wg0_lo = sb("wg0_lo", [P, D], F32R, st)
            wg1 = sb("wg1", [P, D], F32, st)
            bg0_rows = sb("bg0_rows", [P, D], F32, st)
            bg1_rows = sb("bg1_rows", [P, D], F32, st)
            bg0_adj = sb("bg0_adj", [P, T], F32, st)
            bias_nat = sb("bias_nat", [SKIPS * GATES, 2, P], F32, st)
            bias_sum = sb("bias_sum", [SKIPS * GATES, P], F32, st)
            bias = sb("bias", [P, SKIPS * GATES], F32, st)
            bias_half = sb("bias_half", [P, SKIPS * GATES], F32, st)
            x_hi = sb("x_hi", [P, 2, BU * C, D], F32R, st)
            x_lo = sb("x_lo", [P, 2, BU * C, D], F32R, st)
            ax_hi = sb("ax_hi", [P, 2, UNIT], F32R, st)
            ax_lo = sb("ax_lo", [P, 2, UNIT], F32R, st)
            h1b = sb("h1b", [P, 2, UNIT], F32, st)
            h1 = sb("h1", [P, 2, UNIT], F32, st)
            hw = sb("hw", [P, 2, BU * C, D], F32, st)
            hw_hi = sb("hw_hi", [P, 2, BU * C, D], F32R, st)
            hw_lo = sb("hw_lo", [P, 2, BU * C, D], F32R, st)
            gate = sb("gate", [P, 2, GATES, UNIT], F32, st)
            cell = sb("cell", [P, 2, UNIT], F32, st)
            hid = sb("hid", [P, 2, UNIT], F32, st)
            cell_t, incr, kept = h1b, h1, hw[:].rearrange("p s c d -> p s (c d)")
            hid_hi, hid_lo = ax_hi, ax_lo
            w_nat = gate[:].rearrange("p s g u -> p (s g u)").rearrange(
                "p (w l g k) -> p w l g k", w=2, l=SKIPS, g=GATES)

            bank = st.enter_context(nc.psum_tensor("bank", [P, 8, UNIT], F32))

            wih_loaded = sem("wih_loaded", st)
            whh_loaded = sem("whh_loaded", st)
            wg0_loaded = sem("wg0_loaded", st)
            wg1_loaded = sem("wg1_loaded", st)
            bg_loaded = sem("bg_loaded", st)
            bias_loaded = sem("bias_loaded", st)
            adj_t = sem("adj_t", st)
            adjT_made = sem("adjT_made", st)
            adjT_hi_made = sem("adjT_hi_made", st)
            wg0_made = sem("wg0_made", st)
            bias_summed = sem("bias_summed", st)
            bias_t = sem("bias_t", st)
            bias_made = sem("bias_made", st)
            bg0_ps = sem("bg0_ps", st)
            bg0_made = sem("bg0_made", st)
            w_t = sem("w_t", st)
            w_hi_made = sem("w_hi_made", st)
            w_lo_made = sem("w_lo_made", st)
            s_xh = sem("s_xh", st)
            s_xl = sem("s_xl", st)
            s_ax = sem("s_ax", st)
            s_axh = sem("s_axh", st)
            s_axl = sem("s_axl", st)
            s_h1p = sem("s_h1p", st)
            s_h1b = sem("s_h1b", st)
            s_h1 = sem("s_h1", st)
            s_hwp = sem("s_hwp", st)
            s_hw = sem("s_hw", st)
            s_hwh = sem("s_hwh", st)
            s_hwl = sem("s_hwl", st)
            s_h2p = sem("s_h2p", st)
            s_hh = sem("s_hh", st)
            s_hl = sem("s_hl", st)
            pre_done = [sem(f"pre_done{s}", st) for s in range(2)]
            gate_done = [sem(f"gate_done{s}", st) for s in range(2)]
            incr_done = [sem(f"incr_done{s}", st) for s in range(2)]
            kept_done = [sem(f"kept_done{s}", st) for s in range(2)]
            cell_done = [sem(f"cell_done{s}", st) for s in range(2)]
            tanh_done = [sem(f"tanh_done{s}", st) for s in range(2)]
            hid_done = [sem(f"hid_done{s}", st) for s in range(2)]
            hi_done = [sem(f"hi_done{s}", st) for s in range(2)]
            lo_done = [sem(f"lo_done{s}", st) for s in range(2)]

            PSUM_AX, PSUM_H1, PSUM_HW, PSUM_H2 = 0, 2, 4, 6

            BATCHES4 = 4
            UNITS_OF = {1: TOK // UNIT, 2: TOK // 2 // UNIT, 3: B // BATCHES4, 4: TOK // 4 // UNIT}
            WIN3 = T // 3
            N_OF = {1: UNIT, 2: UNIT, 3: BATCHES4 * WIN3, 4: UNIT}
            ITERS = {p: UNITS_OF[p] // 2 for p in UNITS_OF}
            GATES_OF = {p: 3 + 4 * (p - 1) for p in UNITS_OF}
            GATE_BASE = {p: sum(ITERS[q] * GATES_OF[q] for q in range(1, p)) for p in UNITS_OF}
            STEP_BASE = {p: sum(ITERS[q] * q for q in range(1, p)) for p in UNITS_OF}
            LATER_BASE = {p: sum(ITERS[q] * (q - 1) for q in range(1, p)) for p in UNITS_OF}
            ORDER0 = [2, 0, 3]
            ORDER = [2, 0, 1, 3]

            def tokens(h, p, unit, t):
                if p == 1:
                    return h[:, bass.ds(unit * UNIT, UNIT)]
                if p == 3:
                    v = h[:].rearrange("q (b t) -> q t b", t=T)
                    return v[:, t:t + 3 * (WIN3 - 1) + 1:3, bass.ds(unit * BATCHES4, BATCHES4)]
                v = h[:].rearrange("q (w t) -> q w t", t=p)
                return v[:, bass.ds(unit * UNIT, UNIT), t]

            def cut(ap, p):
                if p != 3:
                    return ap
                return ap[:, 0:N_OF[3]].rearrange("q (w b) -> q w b", b=BATCHES4)

            def gates_before(p, seq, t):
                return GATE_BASE[p] + seq * GATES_OF[p] + (0 if t == 0 else 3 + 4 * (t - 1))

            def steps_before(p, seq, t):
                return STEP_BASE[p] + seq * p + t

            def later_steps_before(p, seq, t):
                return LATER_BASE[p] + seq * (p - 1) + t - 1

            def graph_rounds(eng, graph_round):
                for r in range(3):
                    graph_round(r, r % 2)
                with eng.Fori(0, (UNITS - 6) // 2) as it:
                    graph_round(it * 2 + 3, 1)
                    graph_round(it * 2 + 4, 0)
                for r in range(UNITS - 3, UNITS + 1):
                    graph_round(r, r % 2)

            def lstm_steps(eng, step):
                for seq in range(2):
                    for slot in range(2):
                        step(1, seq, slot, 0)
                with eng.Fori(1, ITERS[1] // 2) as it:
                    for k in range(2):
                        for slot in range(2):
                            step(1, it * 2 + k, slot, 0)
                for p in range(2, SKIPS + 1):
                    with eng.Fori(0, ITERS[p]) as it:
                        for t in range(p):
                            for slot in range(2):
                                step(p, it, slot, t)

            def there(n):
                return not isinstance(n, int) or 0 <= n < UNITS

            block = st.enter_context(nc.Block())

            @block.sync
            def _(sp):
                per = CH // len(x_loaded)
                sp.dma_start(adj_nat[:], adj.rearrange("(c p) s -> p c s", p=P)).then_inc(adj_loaded, 16)
                sp.dma_start(res[:, 0:per, :], x_v[:, 0:per, :]).then_inc(x_loaded[0], 16)
                sp.dma_start(w_nat[:, 0], Wih.rearrange("l (g r) k -> r l g k", r=P)).then_inc(wih_loaded, 16)
                sp.dma_start(w_nat[:, 1], Whh.rearrange("l (g r) k -> r l g k", r=P)).then_inc(whh_loaded, 16)
                for k in range(1, len(x_loaded)):
                    sp.dma_start(res[:, k * per:(k + 1) * per, :],
                                 x_v[:, k * per:(k + 1) * per, :]).then_inc(x_loaded[k], 16)
                sp.dma_start(wqkv[:], Wqkv).then_inc(wqkv_loaded, 16)
                sp.wait_ge(wqkv_loaded, 16)

            @block.gpsimd
            def _(pool):
                pool.memset(ident[:], 0.0).then_inc(ident_made, 1)
                pool.memset(head_rows[:], 1.0).then_inc(rows_made, 1)
                pool.wait_ge(ident_made, 1)
                pool.affine_select(out=ident[:], in_=ident[:], compare_op=ALU.not_equal, fill=1.0, base=0,
                                   pattern=[[-1, P]], channel_multiplier=1).then_inc(ident_made, 1)
                pool.wait_ge(rows_made, 1)
                pool.affine_select(out=head_rows[:], in_=head_rows[:], compare_op=ALU.is_ge, fill=0.0, base=0,
                                   pattern=[[-HD, HEADS]], channel_multiplier=1).then_inc(rows_made, 1)
                pool.wait_ge(rows_made, 2)
                pool.affine_select(out=head_rows[:], in_=head_rows[:], compare_op=ALU.is_ge, fill=0.0, base=HD - 1,
                                   pattern=[[HD, HEADS]], channel_multiplier=-1).then_inc(rows_made, 1)

                def split_x(n, slot):
                    if not there(n):
                        return
                    pool.wait_ge(s_xh, n + 1)
                    wait(pool, s_ax, n - 1)
                    pool.tensor_tensor(x_lo[:, slot], res[:, bass.ds(n * BU * C, BU * C), :],
                                       x_hi[:, slot].bitcast(F32), ALU.subtract).then_inc(s_xl, 1)

                def split_hw(n, slot):
                    if not there(n):
                        return
                    pool.wait_ge(s_hwh, n + 1)
                    wait(pool, s_h2p, n - 1)
                    pool.tensor_tensor(hw_lo[:, slot], hw[:, slot], hw_hi[:, slot].bitcast(F32),
                                       ALU.subtract).then_inc(s_hwl, 1)

                def graph_round(r, slot):
                    split_x(r + 2, slot)
                    split_hw(r, slot)

                split_x(0, 0)
                split_x(1, 1)
                graph_rounds(pool, graph_round)

                def step(p, seq, slot, t):
                    n = steps_before(p, seq, t)
                    unit = seq * 2 + slot
                    pool.wait_ge(hi_done[slot], n + 1)
                    full = cut(hid[:, slot], p)
                    if t == p - 1:
                        dst, hi = tokens(h_lo, p, unit, t), tokens(h_hi, p, unit, t)
                    else:
                        dst, hi = cut(hid_lo[:, slot], p), cut(hid_hi[:, slot], p)
                    pool.tensor_tensor(dst, full, hi.bitcast(F32), ALU.subtract).then_inc(lo_done[slot], 1)

                lstm_steps(pool, step)

            @block.scalar
            def _(act):
                act.dma_start(wg0[:], Wg0).then_inc(wg0_loaded, 16)
                act.dma_start(bg0_rows[:], bg0.partition_broadcast(P)).then_inc(bg_loaded, 16)
                act.dma_start(wg1[:], Wg1).then_inc(wg1_loaded, 16)
                act.dma_start(bg1_rows[:], bg1.partition_broadcast(P)).then_inc(bg_loaded, 16)
                act.dma_start(bias_nat[:, 0, :], bih.rearrange("l (g r) -> (l g) r", r=P)).then_inc(bias_loaded, 16)
                act.dma_start(bias_nat[:, 1, :], bhh.rearrange("l (g r) -> (l g) r", r=P)).then_inc(bias_loaded, 16)

                def round_x(n, slot):
                    if not there(n):
                        return
                    if isinstance(n, int) and n < 2:
                        act.wait_ge(x_loaded[0], 16)
                    wait(act, s_ax, n - 1)
                    wait(act, s_xl, n - 1)
                    act.activation(x_hi[:, slot], res[:, bass.ds(n * BU * C, BU * C), :],
                                   ACT.Copy).then_inc(s_xh, 1)

                def graph_round(r, slot):
                    nxt = 1 - slot
                    if there(r + 1):
                        n = r + 1
                        act.wait_ge(s_ax, n + 1)
                        wait(act, s_h1p, n - 1)
                        wait(act, s_axl, n - 1)
                        act.activation(ax_hi[:, nxt], bank[:, PSUM_AX + nxt, :], ACT.Copy).then_inc(s_axh, 1)
                    round_x(r + 2, slot)
                    if there(r):
                        act.wait_ge(s_hw, r + 1)
                        wait(act, s_h2p, r - 1)
                        wait(act, s_hwl, r - 1)
                        act.activation(hw_hi[:, slot], hw[:, slot], ACT.Copy).then_inc(s_hwh, 1)
                    if there(r - 1):
                        n = r - 1
                        act.wait_ge(s_h2p, n + 1)
                        act.activation(h_hi[:, bass.ds(n * UNIT, UNIT)], bank[:, PSUM_H2 + nxt, :],
                                       ACT.Relu).then_inc(s_hh, 1)
                    if there(r + 1):
                        n = r + 1
                        act.wait_ge(s_h1b, n + 1)
                        wait(act, s_hwp, n - 1)
                        act.activation(h1[:, nxt], h1b[:, nxt], ACT.Relu).then_inc(s_h1, 1)

                act.wait_ge(adjT_made, 1)
                act.activation(adjT_hi[:].rearrange("p c t -> p (c t)"), bank[:, 7, :],
                               ACT.Copy).then_inc(adjT_hi_made, 1)
                round_x(0, 0)
                for k in range(2 * SKIPS):
                    l, w = k // 2, k % 2
                    act.wait_ge(w_t, k + 1)
                    act.activation(w_hi[:, l, w, :], bank[:, k % 6, :], ACT.Copy,
                                   scale=1.0 if k == 0 else 0.5).then_inc(w_hi_made, 1)
                for k in range(1, len(x_loaded)):
                    act.wait_ge(x_loaded[k], 16)
                graph_round(-1, 1)
                graph_rounds(act, graph_round)

                act.wait_ge(bias_made, 2)

                def step(p, seq, slot, t):
                    g0, n = gates_before(p, seq, t), steps_before(p, seq, t)
                    wait(act, hid_done[slot], n)
                    for k, g in enumerate(ORDER if t else ORDER0):
                        act.wait_ge(pre_done[slot], g0 + k + 1)
                        b = (bias if g == 2 else bias_half)[:, (p - 1) * GATES + g:(p - 1) * GATES + g + 1]
                        act.activation(gate[:, slot, g, 0:N_OF[p]], bank[:, slot * GATES + g, 0:N_OF[p]], ACT.Tanh,
                                       bias=b, scale=1.0 if g == 2 else 0.5).then_inc(gate_done[slot], 1)
                    act.wait_ge(cell_done[slot], n + 1)
                    act.activation(cell_t[:, slot, 0:N_OF[p]], cell[:, slot, 0:N_OF[p]], ACT.Tanh,
                                   scale=0.5).then_inc(tanh_done[slot], 1)

                lstm_steps(act, step)

            @block.vector
            def _(dve):
                dve.wait_ge(adj_loaded, 16)
                dve.tensor_scalar(mask[:], adj_nat[:], 0.0, MASKED, ALU.is_equal, ALU.mult).then_inc(mask_made, 1)
                dve.wait_ge(ident_made, 2)
                dve.tensor_copy(ident_bf[:], ident[:]).then_inc(ident_bf_made, 1)
                dve.wait_ge(adj_t, 1)
                flat = adjT[:].rearrange("p c t -> p (c t)")
                dve.tensor_copy(flat, bank[:, 7, :]).then_inc(adjT_made, 1)
                dve.wait_ge(adjT_made, 1)
                dve.wait_ge(adjT_hi_made, 1)
                dve.tensor_tensor(adjT_lo[:], adjT[:], adjT_hi[:].bitcast(F32), ALU.subtract).then_inc(adjT_made, 1)
                dve.wait_ge(wg0_loaded, 16)
                dve.tensor_copy(wg0_hi[:], wg0[:]).then_inc(wg0_made, 1)
                dve.wait_ge(wg0_made, 1)
                dve.tensor_tensor(wg0_lo[:], wg0[:], wg0_hi[:].bitcast(F32), ALU.subtract).then_inc(wg0_made, 1)
                dve.wait_ge(bg0_ps, 1)
                dve.tensor_copy(bg0_adj[:], bank[:, 7, 0:T]).then_inc(bg0_made, 1)
                dve.wait_ge(bias_loaded, 32)
                dve.tensor_tensor(bias_sum[:], bias_nat[:, 0, :], bias_nat[:, 1, :], ALU.add).then_inc(bias_summed, 1)
                dve.wait_ge(bias_t, 1)
                dve.tensor_copy(bias[:], bank[:, 6, 0:SKIPS * GATES]).then_inc(bias_made, 1)
                dve.tensor_scalar(bias_half[:], bank[:, 6, 0:SKIPS * GATES], 0.5, None, ALU.mult).then_inc(bias_made, 1)
                for k in range(2 * SKIPS):
                    l, w = k // 2, k % 2
                    dve.wait_ge(w_hi_made, k + 1)
                    dve.scalar_tensor_tensor(w_lo[:, l, w, :], bank[:, k % 6, :], 1.0 if k == 0 else 0.5,
                                             w_hi[:, l, w, :].bitcast(F32), ALU.mult,
                                             ALU.subtract).then_inc(w_lo_made, 1)

                bg0_b = bg0_adj[:].unsqueeze(1).broadcast_to([P, BU, T])
                bg1_b = bg1_rows[:].unsqueeze(1).broadcast_to([P, BU * C, D])
                dve.wait_ge(bg_loaded, 32)
                dve.wait_ge(bg0_made, 1)

                def graph_round(r, slot):
                    nxt = 1 - slot
                    if there(r + 1):
                        n = r + 1
                        dve.wait_ge(s_axh, n + 1)
                        wait(dve, s_h1p, n - 1)
                        dve.tensor_tensor(ax_lo[:, nxt], bank[:, PSUM_AX + nxt, :], ax_hi[:, nxt].bitcast(F32),
                                          ALU.subtract).then_inc(s_axl, 1)
                    if there(r):
                        dve.wait_ge(s_hwp, r + 1)
                        wait(dve, s_hwh, r - 1)
                        wait(dve, s_hwl, r - 1)
                        dve.tensor_tensor(hw[:, slot], bank[:, PSUM_HW + slot, :].rearrange("p (c d) -> p c d", d=D),
                                          bg1_b, ALU.add).then_inc(s_hw, 1)
                    if there(r - 1):
                        n = r - 1
                        dve.wait_ge(s_hh, n + 1)
                        dve.scalar_tensor_tensor(h_lo[:, bass.ds(n * UNIT, UNIT)], bank[:, PSUM_H2 + nxt, :], 0.0,
                                                 h_hi[:, bass.ds(n * UNIT, UNIT)].bitcast(F32), ALU.max,
                                                 ALU.subtract).then_inc(s_hl, 1)
                    if there(r + 1):
                        n = r + 1
                        dve.wait_ge(s_h1p, n + 1)
                        wait(dve, s_h1, n - 1)
                        dve.tensor_tensor(h1b[:, nxt].rearrange("p (b t) -> p b t", t=T),
                                          bank[:, PSUM_H1 + nxt, :].rearrange("p (b t) -> p b t", t=T),
                                          bg0_b, ALU.add).then_inc(s_h1b, 1)

                graph_round(-1, 1)
                graph_rounds(dve, graph_round)

                def step(p, seq, slot, t):
                    g0, n = gates_before(p, seq, t), steps_before(p, seq, t)
                    unit = seq * 2 + slot
                    w = slice(0, N_OF[p])
                    g_i, g_f, g_g, g_o = (gate[:, slot, g, w] for g in range(GATES))
                    dve.wait_ge(gate_done[slot], g0 + 2)
                    if t == 0:
                        wait(dve, tanh_done[slot], n)
                        dve.scalar_tensor_tensor(cell[:, slot, w], g_i, 1.0, g_g, ALU.add,
                                                 ALU.mult).then_inc(cell_done[slot], 1)
                        dve.wait_ge(gate_done[slot], g0 + 3)
                    else:
                        m = later_steps_before(p, seq, t)
                        dve.scalar_tensor_tensor(incr[:, slot, w], g_i, 1.0, g_g, ALU.add,
                                                 ALU.mult).then_inc(incr_done[slot], 1)
                        dve.wait_ge(gate_done[slot], g0 + 3)
                        dve.scalar_tensor_tensor(kept[:, slot, w], g_f, 1.0, cell[:, slot, w], ALU.add,
                                                 ALU.mult).then_inc(kept_done[slot], 1)
                        dve.wait_ge(incr_done[slot], m + 1)
                        dve.wait_ge(kept_done[slot], m + 1)
                        dve.scalar_tensor_tensor(cell[:, slot, w], kept[:, slot, w], 0.5, incr[:, slot, w], ALU.mult,
                                                 ALU.add).then_inc(cell_done[slot], 1)
                        dve.wait_ge(gate_done[slot], g0 + 4)
                    dve.wait_ge(tanh_done[slot], n + 1)
                    wait(dve, lo_done[slot], n)
                    dve.scalar_tensor_tensor(hid[:, slot, w], g_o, 1.0, cell_t[:, slot, w], ALU.add,
                                             ALU.mult).then_inc(hid_done[slot], 1)
                    dve.wait_ge(hid_done[slot], n + 1)
                    dst = tokens(h_hi, p, unit, t) if t == p - 1 else cut(hid_hi[:, slot], p)
                    dve.tensor_copy(dst, cut(hid[:, slot], p)).then_inc(hi_done[slot], 1)

                lstm_steps(dve, step)

            @block.tensor
            def _(pe):
                def product3(out_ap, lhs_hi, lhs_lo, rhs_hi, rhs_lo, start=True, stop=True):
                    pe.matmul(out_ap, lhs_hi, rhs_hi, start=start, stop=False)
                    pe.matmul(out_ap, lhs_hi, rhs_lo, start=False, stop=False)
                    return pe.matmul(out_ap, lhs_lo, rhs_hi, start=False, stop=stop)

                pe.wait_ge(adj_loaded, 16)
                pe.wait_ge(ident_made, 2)
                for s in range(C):
                    for t in range(C):
                        last = pe.transpose(bank[:, 7, s * T + t * P:s * T + (t + 1) * P],
                                            adj_nat[:, t, s * P:(s + 1) * P], ident[:])
                last.then_inc(adj_t, 1)
                pe.wait_ge(adjT_made, 2)
                pe.wait_ge(bg_loaded, 32)
                for s in range(C):
                    last = pe.matmul(bank[:, 7, 0:T], bg0_rows[:], adjT[:, s, :], start=(s == 0), stop=(s == C - 1))
                last.then_inc(bg0_ps, 1)
                pe.wait_ge(bias_summed, 1)
                n_b = SKIPS * GATES
                pe.transpose(bank[:, 6, 0:n_b], bias_sum[:], ident[0:n_b, 0:n_b]).then_inc(bias_t, 1)
                pe.wait_ge(wih_loaded, 16)
                pe.wait_ge(whh_loaded, 16)
                for k in range(2 * SKIPS):
                    l, w = k // 2, k % 2
                    if k >= 6:
                        pe.wait_ge(w_lo_made, k - 5)
                    for g in range(GATES):
                        last = pe.transpose(bank[:, k % 6, g * P:(g + 1) * P], w_nat[:, w, l, g, :], ident[:])
                    last.then_inc(w_t, 1)
                pe.wait_ge(w_lo_made, 2 * SKIPS)
                pe.wait_ge(wg0_made, 2)
                pe.wait_ge(wg1_loaded, 16)
                pe.wait_ge(bg0_made, 1)
                pe.wait_ge(bias_made, 2)

                def adj_x(n, slot):
                    pe.wait_ge(s_xh, n + 1)
                    pe.wait_ge(s_xl, n + 1)
                    wait(pe, s_axl, n - 1)
                    for b in range(BU):
                        o = bank[:, PSUM_AX + slot, b * T:(b + 1) * T]
                        for s in range(C):
                            last = product3(o, x_hi[:, slot, b * C + s, :], x_lo[:, slot, b * C + s, :],
                                            adjT_hi[:, s, :], adjT_lo[:, s, :], s == 0, s == C - 1)
                    last.then_inc(s_ax, 1)

                def layer1(n, slot):
                    pe.wait_ge(s_axh, n + 1)
                    pe.wait_ge(s_axl, n + 1)
                    wait(pe, s_h1b, n - 1)
                    product3(bank[:, PSUM_H1 + slot, :], wg0_hi[:], wg0_lo[:], ax_hi[:, slot],
                             ax_lo[:, slot]).then_inc(s_h1p, 1)

                def weight2(n, slot):
                    pe.wait_ge(s_h1, n + 1)
                    wait(pe, s_hw, n - 1)
                    for c in range(BU * C):
                        last = pe.matmul(bank[:, PSUM_HW + slot, c * D:(c + 1) * D], h1[:, slot, c * P:(c + 1) * P],
                                         wg1[:], start=True, stop=True)
                    last.then_inc(s_hwp, 1)

                def layer2(n, slot):
                    pe.wait_ge(s_hwh, n + 1)
                    pe.wait_ge(s_hwl, n + 1)
                    wait(pe, s_hl, n - 1)
                    for b in range(BU):
                        o = bank[:, PSUM_H2 + slot, b * T:(b + 1) * T]
                        for s in range(C):
                            last = product3(o, hw_hi[:, slot, b * C + s, :], hw_lo[:, slot, b * C + s, :],
                                            adjT_hi[:, s, :], adjT_lo[:, s, :], s == 0, s == C - 1)
                    last.then_inc(s_h2p, 1)

                def graph_round(r, slot):
                    nxt = 1 - slot
                    if there(r + 1):
                        adj_x(r + 1, nxt)
                    if there(r):
                        weight2(r, slot)
                    if there(r - 1):
                        layer2(r - 1, nxt)
                    if there(r + 1):
                        layer1(r + 1, nxt)

                graph_round(-1, 1)
                graph_rounds(pe, graph_round)
                pe.wait_ge(s_hh, UNITS)
                pe.wait_ge(s_hl, UNITS)

                def step(p, seq, slot, t):
                    g0, n = gates_before(p, seq, t), steps_before(p, seq, t)
                    unit = seq * 2 + slot
                    order = ORDER if t else ORDER0
                    if t == 0 and p == 2:
                        for s in range(2):
                            pe.wait_ge(hi_done[s], STEP_BASE[1] + unit + 1)
                            pe.wait_ge(lo_done[s], STEP_BASE[1] + unit + 1)
                    if t == 0 and p == 3:
                        pe.wait_ge(hi_done[slot], STEP_BASE[2] + (seq + 1) * 2)
                        pe.wait_ge(lo_done[slot], STEP_BASE[2] + (seq + 1) * 2)
                    if t == 0 and p == 4:
                        for s in range(2):
                            pe.wait_ge(hi_done[s], STEP_BASE[3] + (unit + 1) * 3)
                            pe.wait_ge(lo_done[s], STEP_BASE[3] + (unit + 1) * 3)
                    wait(pe, gate_done[slot], g0)
                    x_h, x_l = tokens(h_hi, p, unit, t), tokens(h_lo, p, unit, t)
                    for g in order:
                        cols = slice(g * P, (g + 1) * P)
                        last = product3(cut(bank[:, slot * GATES + g], p), w_hi[:, p - 1, 0, cols],
                                        w_lo[:, p - 1, 0, cols], x_h, x_l, True, t == 0)
                        if t == 0:
                            last.then_inc(pre_done[slot], 1)
                    if t > 0:
                        pe.wait_ge(hi_done[slot], n)
                        pe.wait_ge(lo_done[slot], n)
                        for g in order:
                            cols = slice(g * P, (g + 1) * P)
                            product3(cut(bank[:, slot * GATES + g], p), w_hi[:, p - 1, 1, cols],
                                     w_lo[:, p - 1, 1, cols], cut(hid_hi[:, slot], p), cut(hid_lo[:, slot], p),
                                     False, True).then_inc(pre_done[slot], 1)

                lstm_steps(pe, step)

        with ExitStack() as st:
            hsum = sb("hsum", [P, 2, UNIT], F32, st)
            stats = sb("stats", [P, 2, BU * C, 6], F32, st)
            moments = sb("moments", [P, 2, BU * C, 2], F32, st)
            neg_mean = sb("neg_mean", [P, CH], F32, st)
            var = sb("var", [P, CH], F32, st)
            std = sb("std", [P, CH], F32, st)
            quot = sb("quot", [P, CH], F32, st)
            rstd = sb("rstd", [P, CH], F32, st)
            shift = sb("shift", [P, CH], F32, st)
            y_in = sb("y_in", [P, 2, C, D], F32, st)
            yT = sb("yT", [P, 2, T], F32, st)
            qk_hi = sb("qk_hi", [P, 2, 2 * T], F32R, st)
            qk_lo = sb("qk_lo", [P, 2, 2 * T], F32R, st)
            kp_hi = sb("kp_hi", [P, 2, HEADS, T], F32R, st)
            kp_lo = sb("kp_lo", [P, 2, HEADS, T], F32R, st)
            v = sb("v", [P, 2, C, D], F32, st)
            neg_max = sb("neg_max", [P, 2, C * HEADS], F32, st)
            exp_bias = sb("exp_bias", [P, 2, C * HEADS], F32, st)
            prob = sb("prob", [P, 2, C, HEADS, T], F32, st)
            prob_sum = sb("prob_sum", [P, 2, C * HEADS], F32, st)
            inv_sum = sb("inv_sum", [P, 2, C * HEADS], F32, st)
            probT = sb("probT", [P, HEADS, C, T], F32, st)
            oT = sb("oT", [P, T], F32, st)
            attn = sb("attn", [P, 2, C, D], F32, st)

            bank = st.enter_context(nc.psum_tensor("bank2", [P, 8, UNIT], F32))
            SCORE_BANKS = [(0, 0), (1, 0), (0, 1), (1, 1)]
            PSUM_PT, PSUM_QKV, PSUM_O = 4, 6, 7

            s_hsum = sem("s_hsum", st)
            s_hT = sem("s_hT", st)
            s_y = sem("s_y", st)
            s_stats = sem("s_stats", st)
            s_moments = sem("s_moments", st)
            var_made = sem("var_made", st)
            std_made = sem("std_made", st)
            rstd_steps = sem("rstd_steps", st)
            normed = sem("normed", st)
            y_staged = [sem(f"y_staged{s}", st) for s in range(2)]
            s_yT = sem("s_yT", st)
            yT_made = sem("yT_made", st)
            s_qk = sem("s_qk", st)
            qk_hi_made = sem("qk_hi_made", st)
            qk_lo_made = sem("qk_lo_made", st)
            kp_made = sem("kp_made", st)
            s_v = sem("s_v", st)
            v_made = sem("v_made", st)
            s_scores = sem("s_scores", st)
            max_made = sem("max_made", st)
            bias_ready = sem("bias_ready", st)
            exp_done = sem("exp_done", st)
            s_probT = sem("s_probT", st)
            probT_dve = sem("probT_dve", st)
            probT_act = sem("probT_act", st)
            s_o = sem("s_o", st)
            oT_made = sem("oT_made", st)
            s_oT = sem("s_oT", st)
            inv_made = sem("inv_made", st)
            attn_made = sem("attn_made", st)
            sum_made = sem("sum_made", st)
            stats2 = sem("stats2", st)
            moments2 = sem("moments2", st)
            out_written = sem("out_written", st)

            PAIR = HEADS // 2

            def batch_rounds(eng, batch_round):
                for r in range(-1, 3):
                    batch_round(r, r % 2)
                with eng.Fori(0, (B - 4) // 2) as it:
                    batch_round(it * 2 + 3, 1)
                    batch_round(it * 2 + 4, 0)
                for r in range(B - 1, B + 2):
                    batch_round(r, r % 2)

            def here(n):
                return not isinstance(n, int) or 0 <= n < B

            def wait_apart(eng, sem, value):
                eng.wait_ge(ident_made, 2)
                eng.wait_ge(sem, value)

            def norm_scales(dve, base):
                dve.wait_ge(std_made, base + 1)
                dve.reciprocal(quot[:], std[:]).then_inc(rstd_steps, 1)
                dve.wait_ge(rstd_steps, 6 * base + 1)
                dve.tensor_tensor(rstd[:], quot[:], var[:], ALU.mult).then_inc(rstd_steps, 1)
                dve.wait_ge(rstd_steps, 6 * base + 2)
                dve.tensor_tensor(quot[:], rstd[:], std[:], ALU.add).then_inc(rstd_steps, 1)
                dve.wait_ge(rstd_steps, 6 * base + 3)
                dve.reciprocal(std[:], quot[:]).then_inc(rstd_steps, 1)
                dve.wait_ge(rstd_steps, 6 * base + 4)
                dve.tensor_scalar(rstd[:], std[:], 2.0, None, ALU.mult).then_inc(rstd_steps, 1)
                dve.wait_ge(rstd_steps, 6 * base + 5)
                dve.scalar_tensor_tensor(shift[:], neg_mean[:], 1.0, rstd[:], ALU.mult,
                                         ALU.mult).then_inc(rstd_steps, 1)

            def norm_chunk(eng, chunk, done):
                ap = res[:, bass.ds(chunk, 1), :]
                eng.tensor_scalar(ap, ap, rstd[:, bass.ds(chunk, 1)], shift[:, bass.ds(chunk, 1)], ALU.mult,
                                  ALU.add).then_inc(done, 1)

            block = st.enter_context(nc.Block())

            @block.sync
            def _(sp):
                sp.wait_ge(normed, CH)

                def batch_round(r, slot):
                    if here(r + 1):
                        n = r + 1
                        wait(sp, s_yT, n - 1)
                        sp.dma_start(y_in[:, 1 - slot], res[:, bass.ds(n * C, C), :]).then_inc(y_staged[1 - slot], 16)

                batch_rounds(sp, batch_round)
                per = CH // 8
                for k in range(8):
                    sp.wait_ge(normed, CH + (k + 1) * per)
                    sp.dma_start(out_v[:, k * per:(k + 1) * per, :],
                                 res[:, k * per:(k + 1) * per, :]).then_inc(out_written, 16)
                sp.wait_ge(out_written, 16 * 8)

            @block.gpsimd
            def _(pool):
                for n in range(2):
                    pool.tensor_tensor(hsum[:, n], h_hi[:, n * UNIT:(n + 1) * UNIT].bitcast(F32),
                                       h_lo[:, n * UNIT:(n + 1) * UNIT].bitcast(F32), ALU.add).then_inc(s_hsum, 1)
                with pool.Fori(1, UNITS // 2) as it:
                    for slot in range(2):
                        n = it * 2 + slot
                        pool.wait_ge(s_hT, n - 1)
                        pool.tensor_tensor(hsum[:, slot], h_hi[:, bass.ds(n * UNIT, UNIT)].bitcast(F32),
                                           h_lo[:, bass.ds(n * UNIT, UNIT)].bitcast(F32), ALU.add).then_inc(s_hsum, 1)
                def batch_round(r, slot):
                    if here(r + 1):
                        n, nxt = r + 1, 1 - slot
                        for pair in range(2):
                            heads = slice(pair * PAIR, (pair + 1) * PAIR)
                            rows = head_rows[:, heads].unsqueeze(2).broadcast_to([P, PAIR, T])
                            for part, made, dst in ((qk_hi, qk_hi_made, kp_hi), (qk_lo, qk_lo_made, kp_lo)):
                                pool.wait_ge(made, n + 1)
                                if pair == 0:
                                    wait(pool, s_scores, (n - 1) * 4)
                                k_b = part[:, nxt, T:2 * T].bitcast(F32).unsqueeze(1).broadcast_to([P, PAIR, T])
                                pool.tensor_tensor(dst[:, nxt, heads, :], k_b, rows, ALU.mult).then_inc(kp_made, 1)

                batch_rounds(pool, batch_round)

            @block.scalar
            def _(act):
                act.wait_ge(var_made, 2 * UNITS)
                act.activation(std[:], var[:], ACT.Sqrt).then_inc(std_made, 1)

                def scores_exp(r, slot, k):
                    if here(r):
                        c, pair = SCORE_BANKS[k]
                        if k == 0:
                            wait(act, s_probT, (r - 1) * 4)
                            wait(act, inv_made, r - 1)
                        act.wait_ge(bias_ready, r * 4 + k + 1)
                        for j in range(PAIR):
                            h = pair * PAIR + j
                            col = c * HEADS + h
                            ins = act.activation(prob[:, slot, c, h, :], bank[:, k, j * T:(j + 1) * T], ACT.Exp,
                                                 bias=exp_bias[:, slot, col:col + 1], scale=SCALE,
                                                 accum_out=prob_sum[:, slot, col:col + 1])
                        ins.then_inc(exp_done, 1)

                def batch_round(r, slot):
                    nxt = 1 - slot
                    if here(r + 1):
                        act.wait_ge(s_yT, r + 2)
                        wait(act, s_v, r)
                        act.activation(yT[:, nxt], bank[:, PSUM_QKV, 0:T], ACT.Copy).then_inc(yT_made, 1)
                    scores_exp(r - 1, nxt, 3)
                    if here(r + 1):
                        act.wait_ge(s_qk, r + 2)
                        wait(act, s_scores, r * 4)
                        wait(act, kp_made, r * 4)
                        act.activation(qk_hi[:, nxt], bank[:, PSUM_QKV, :], ACT.Copy).then_inc(qk_hi_made, 1)
                    scores_exp(r, slot, 0)
                    if here(r - 1):
                        for h in range(2, HEADS):
                            act.wait_ge(s_probT, (r - 1) * 4 + h + 1)
                            wait(act, s_o, r - 1)
                            act.activation(probT[:, h].rearrange("p c t -> p (c t)"), bank[:, PSUM_PT + h % 2, :],
                                           ACT.Copy).then_inc(probT_act, 1)
                    if here(r):
                        act.wait_ge(s_v, r + 1)
                        wait(act, s_o, r - 1)
                        act.activation(v[:, slot].rearrange("p c d -> p (c d)"), bank[:, PSUM_QKV, 0:C * D],
                                       ACT.Copy).then_inc(v_made, 1)
                    scores_exp(r, slot, 1)
                    scores_exp(r, slot, 2)
                    if here(r - 1):
                        act.wait_ge(s_o, r)
                        wait(act, s_oT, r - 1)
                        act.activation(oT[:], bank[:, PSUM_O, 0:T], ACT.Copy).then_inc(oT_made, 1)

                batch_rounds(act, batch_round)
                act.wait_ge(var_made, 2 * UNITS + 2 * B)
                act.activation(std[:], var[:], ACT.Sqrt).then_inc(std_made, 1)

            @block.vector
            def _(dve):
                def keep_moments(chunk, slot, count, done):
                    dve.tensor_scalar(var[:, bass.ds(chunk, count)], moments[:, slot, 0:count, 1], EPS, None,
                                      ALU.add).then_inc(done, 1)
                    dve.tensor_scalar(neg_mean[:, bass.ds(chunk, count)], moments[:, slot, 0:count, 0], -1.0, None,
                                      ALU.mult).then_inc(done, 1)

                def residual(n, slot):
                    chunks = BU * C
                    ap = res[:, bass.ds(n * chunks, chunks), :]
                    dve.wait_ge(s_hT, n + 1)
                    dve.scalar_tensor_tensor(ap, bank[:, PSUM_PT + slot, :].rearrange("p (c d) -> p c d", d=D), 0.5,
                                             ap, ALU.mult, ALU.add).then_inc(s_y, 1)
                    wait_apart(dve, s_y, n + 1)
                    for k in range(chunks):
                        ins = dve.bn_stats(stats[:, slot, k, :], res[:, bass.ds(n * chunks + k, 1), :])
                    ins.then_inc(s_stats, 1)
                    wait_apart(dve, s_stats, n + 1)
                    for k in range(chunks):
                        ins = dve.bn_aggr(moments[:, slot, k, :], stats[:, slot, k, :])
                    ins.then_inc(s_moments, 1)
                    dve.wait_ge(s_moments, n + 1)
                    keep_moments(n * chunks, slot, chunks, var_made)

                residual(0, 0)
                residual(1, 1)
                with dve.Fori(1, UNITS // 2) as it:
                    residual(it * 2, 0)
                    residual(it * 2 + 1, 1)
                dve.wait_ge(var_made, 2 * UNITS)
                norm_scales(dve, 0)
                dve.wait_ge(rstd_steps, 6)
                with dve.Fori(0, CH // 4) as it:
                    for k in range(4):
                        norm_chunk(dve, it * 4 + k, normed)

                def row_max(r, slot, k):
                    if here(r):
                        c, pair = SCORE_BANKS[k]
                        cols = slice(c * HEADS + pair * PAIR, c * HEADS + (pair + 1) * PAIR)
                        dve.wait_ge(s_scores, r * 4 + k + 1)
                        wait(dve, exp_done, (r - 1) * 4)
                        dve.tensor_reduce(neg_max[:, slot, cols], bank[:, k, :].rearrange("p (h t) -> p h t", t=T),
                                          AX.X, ALU.max, negate=True).then_inc(max_made, 1)
                        dve.wait_ge(max_made, r * 4 + k + 1)
                        dve.tensor_scalar(exp_bias[:, slot, cols], neg_max[:, slot, cols], SCALE, None,
                                          ALU.mult).then_inc(bias_ready, 1)

                def batch_round(r, slot):
                    nxt = 1 - slot
                    if here(r - 2):
                        dve.wait_ge(exp_done, (r - 1) * 4)
                        dve.reciprocal(inv_sum[:, slot], prob_sum[:, slot]).then_inc(inv_made, 1)
                    if here(r - 1):
                        for h in range(2):
                            dve.wait_ge(s_probT, (r - 1) * 4 + h + 1)
                            wait(dve, s_o, r - 1)
                            dve.tensor_copy(probT[:, h].rearrange("p c t -> p (c t)"),
                                            bank[:, PSUM_PT + h % 2, :]).then_inc(probT_dve, 1)
                    row_max(r, slot, 0)
                    if here(r + 1):
                        dve.wait_ge(qk_hi_made, r + 2)
                        wait(dve, s_scores, r * 4)
                        wait(dve, kp_made, r * 4)
                        dve.tensor_tensor(qk_lo[:, nxt], bank[:, PSUM_QKV, :], qk_hi[:, nxt].bitcast(F32),
                                          ALU.subtract).then_inc(qk_lo_made, 1)
                    if here(r - 2):
                        n = r - 2
                        dve.wait_ge(s_oT, r - 1)
                        dve.wait_ge(inv_made, r - 1)
                        dve.tensor_tensor(attn[:, slot].rearrange("p c (h d) -> p (c h) d", d=HD),
                                          bank[:, PSUM_O, T:2 * T].rearrange("p (g d) -> p g d", d=HD),
                                          inv_sum[:, slot].unsqueeze(2).broadcast_to([P, C * HEADS, HD]),
                                          ALU.mult).then_inc(attn_made, 1)
                        dve.wait_ge(attn_made, r - 1)
                        ap = res[:, bass.ds(n * C, C), :]
                        dve.tensor_tensor(ap, ap, attn[:, slot], ALU.add).then_inc(sum_made, 1)
                    row_max(r, slot, 1)
                    row_max(r, slot, 2)
                    if here(r - 2):
                        n = r - 2
                        wait_apart(dve, sum_made, r - 1)
                        for c in range(C):
                            ins = dve.bn_stats(stats[:, slot, c, :], res[:, bass.ds(n * C + c, 1), :])
                        ins.then_inc(stats2, 1)
                    if here(r - 2):
                        wait_apart(dve, stats2, r - 1)
                        for c in range(C):
                            ins = dve.bn_aggr(moments[:, slot, c, :], stats[:, slot, c, :])
                        ins.then_inc(moments2, 1)
                    row_max(r, slot, 3)
                    if here(r - 2):
                        dve.wait_ge(moments2, r - 1)
                        keep_moments((r - 2) * C, slot, C, var_made)

                batch_rounds(dve, batch_round)
                dve.wait_ge(var_made, 2 * UNITS + 2 * B)
                norm_scales(dve, 1)
                dve.wait_ge(rstd_steps, 12)
                with dve.Fori(0, CH // 4) as it:
                    for k in range(4):
                        norm_chunk(dve, it * 4 + k, normed)

            @block.tensor
            def _(pe):
                def back_transpose(n, slot):
                    pe.wait_ge(s_hsum, n + 1)
                    wait(pe, s_y, n - 1)
                    for k in range(BU * C):
                        last = pe.transpose(bank[:, PSUM_PT + slot, k * P:(k + 1) * P],
                                            hsum[:, slot, k * P:(k + 1) * P], ident[:])
                    last.then_inc(s_hT, 1)

                back_transpose(0, 0)
                back_transpose(1, 1)
                with pe.Fori(1, UNITS // 2) as it:
                    back_transpose(it * 2, 0)
                    back_transpose(it * 2 + 1, 1)

                def scores(r, slot, k):
                    if here(r):
                        c, pair = SCORE_BANKS[k]
                        heads = slice(pair * PAIR, (pair + 1) * PAIR)
                        wait(pe, exp_done, (r - 1) * 4 + k + 1)
                        pe.matmul(bank[:, k, :], ident_bf[:], mask[:, c, :].unsqueeze(1).broadcast_to([P, PAIR, T]),
                                  start=True, stop=False)
                        pe.wait_ge(qk_lo_made, r + 1)
                        pe.wait_ge(kp_made, r * 4 + 2 * pair + 2)
                        q_hi = qk_hi[:, slot, c * P:(c + 1) * P]
                        q_lo = qk_lo[:, slot, c * P:(c + 1) * P]
                        k_hi, k_lo = (a[:, slot, heads, :].rearrange("p h t -> p (h t)") for a in (kp_hi, kp_lo))
                        pe.matmul(bank[:, k, :], q_hi, k_hi, start=False, stop=False)
                        pe.matmul(bank[:, k, :], q_hi, k_lo, start=False, stop=False)
                        pe.matmul(bank[:, k, :], q_lo, k_hi, start=False, stop=True).then_inc(s_scores, 1)

                def prob_transposes(n, slot, h):
                    if here(n):
                        if h < 2:
                            pe.wait_ge(exp_done, n * 4 + 2)
                            wait(pe, probT_act, n * 2 - 1 + h)
                        else:
                            pe.wait_ge(exp_done, n * 4 + 4)
                            pe.wait_ge(probT_dve, n * 2 + h - 1)
                        for kc in range(C):
                            for c in range(C):
                                last = pe.transpose(bank[:, PSUM_PT + h % 2, kc * T + c * P:kc * T + (c + 1) * P],
                                                    prob[:, slot, c, h, kc * P:(kc + 1) * P], ident[:])
                        last.then_inc(s_probT, 1)

                def batch_round(r, slot):
                    nxt = 1 - slot
                    if here(r + 1):
                        pe.wait_ge(y_staged[nxt], 8 * (r + 1) + (8 if nxt else 16))
                        wait(pe, qk_lo_made, r + 1)
                        wait(pe, v_made, r)
                        for c in range(C):
                            last = pe.transpose(bank[:, PSUM_QKV, c * P:(c + 1) * P], y_in[:, nxt, c, :], ident[:])
                        last.then_inc(s_yT, 1)
                    prob_transposes(r - 1, nxt, 0)
                    prob_transposes(r - 1, nxt, 1)
                    scores(r, slot, 0)
                    if here(r - 2):
                        pe.wait_ge(oT_made, r - 1)
                        for c in range(C):
                            last = pe.transpose(bank[:, PSUM_O, T + c * P:T + (c + 1) * P], oT[:, c * P:(c + 1) * P],
                                                ident[:])
                        last.then_inc(s_oT, 1)
                    if here(r + 1):
                        pe.wait_ge(yT_made, r + 2)
                        for j in range(2):
                            last = pe.matmul(bank[:, PSUM_QKV, j * T:(j + 1) * T], wqkv[:, j * D:(j + 1) * D], yT[:, nxt],
                                             start=True, stop=True)
                        last.then_inc(s_qk, 1)
                    prob_transposes(r - 1, nxt, 2)
                    prob_transposes(r - 1, nxt, 3)
                    scores(r, slot, 1)
                    if here(r):
                        if here(r + 1):
                            pe.wait_ge(qk_lo_made, r + 2)
                        for c in range(C):
                            last = pe.matmul(bank[:, PSUM_QKV, c * D:(c + 1) * D], yT[:, slot, c * P:(c + 1) * P],
                                             wqkv[:, 2 * D:3 * D], start=True, stop=True)
                        last.then_inc(s_v, 1)
                    scores(r, slot, 2)
                    if here(r - 1):
                        pe.wait_ge(probT_dve, r * 2)
                        pe.wait_ge(probT_act, r * 2)
                        pe.wait_ge(v_made, r)
                        wait(pe, attn_made, r - 1)
                        for kc in range(C):
                            for h in range(HEADS):
                                rows = slice(h * HD, (h + 1) * HD)
                                last = pe.matmul(bank[rows, PSUM_O, 0:T], v[:, nxt, kc, rows], probT[:, h, kc, :],
                                                 start=(kc == 0), stop=(kc == C - 1))
                        last.then_inc(s_o, 1)
                    scores(r, slot, 3)

                batch_rounds(pe, batch_round)


_INS = ['x', 'adj', 'L0_gnn_Wg0', 'L0_gnn_bg0', 'L0_gnn_Wg1', 'L0_gnn_bg1', 'L0_gnn_Wih', 'L0_gnn_Whh',
        'L0_gnn_bih', 'L0_gnn_bhh', 'L1_gnn_W']
_OUTS = [((32, 256, 128), 'float32')]


def kernel(**inputs):
    import numpy as _np
    import concourse.bacc as _bacc
    from concourse import mybir as _mybir
    from concourse.bass_utils import run_bass_kernel_spmd as _run

    nc = _bacc.Bacc("TRN2", target_bir_lowering=False, num_devices=1)
    arrays, args = {}, []
    for name in _INS:
        a = _np.ascontiguousarray(inputs[name])
        arrays[f"in_{name}_dram"] = a
        args.append(nc.dram_tensor(f"in_{name}_dram", a.shape, _mybir.dt.from_np(a.dtype), kind="ExternalInput").ap())
    for i, (shape, dtype) in enumerate(_OUTS):
        dt = _mybir.dt.from_np(_np.dtype(dtype))
        args.append(nc.dram_tensor(f"out_{i}_dram", shape, dt, kind="ExternalOutput").ap())
    graph_kernel(nc, *args)
    r = _run(nc, [arrays], core_ids=[0])
    got = tuple(r.results[0][f"out_{i}_dram"] for i in range(len(_OUTS)))
    return got[0]
```

```python
from contextlib import ExitStack

import concourse.bass as bass
from concourse import mybir
from concourse.alu_op_type import AluOpType as ALU

F32 = mybir.dt.float32
F32R = mybir.dt.float32r
BF16 = mybir.dt.bfloat16
ACT = mybir.ActivationFunctionType
AX = mybir.AxisListType

P = 128
MASKED = -1.0e30
EPS = 1e-05


def wait(eng, sem, value):
    if isinstance(value, int) and value <= 0:
        return
    eng.wait_ge(sem, value)


def graph_kernel(nc, x, adj, Wg0, bg0, Wg1, bg1, Wih, Whh, bih, bhh, Wqkv, out):
    B, T, D = x.shape
    SKIPS, G4, _ = Wih.shape
    GATES = G4 // P
    TOK = B * T
    UNIT = 512
    UNITS = TOK // UNIT
    BU = UNIT // T
    C = T // P
    CH = TOK // P
    HEADS = 4
    HD = D // HEADS
    SCALE = float(HD) ** -0.5
    assert D == P and T == 256 and GATES == 4 and SKIPS == 4

    x_v = x.rearrange("b (c p) d -> p (b c) d", p=P)
    out_v = out.rearrange("b (c p) d -> p (b c) d", p=P)

    with ExitStack() as top:
        def sb(name, shape, dt, ctx=top):
            return ctx.enter_context(nc.sbuf_tensor(name, shape, dt))

        def sem(name, ctx=top):
            return ctx.enter_context(nc.semaphore(name))

        res = sb("res", [P, CH, D], F32)
        h_hi = sb("h_hi", [P, TOK], F32R)
        h_lo = sb("h_lo", [P, TOK], F32R)
        ident = sb("ident", [P, P], F32)
        ident_bf = sb("ident_bf", [P, P], BF16)
        adj_nat = sb("adj_nat", [P, C, T], F32)
        mask = sb("mask", [P, C, T], BF16)
        wqkv = sb("wqkv", [P, 3 * D], F32)
        head_rows = sb("head_rows", [P, HEADS], F32)

        x_loaded = [sem(f"x_loaded{k}") for k in range(4)]
        ident_made = sem("ident_made")
        ident_bf_made = sem("ident_bf_made")
        rows_made = sem("rows_made")
        mask_made = sem("mask_made")
        adj_loaded = sem("adj_loaded")
        wqkv_loaded = sem("wqkv_loaded")

        with ExitStack() as st:
            w_hi = sb("w_hi", [P, SKIPS, 2, G4], F32R, st)
            w_lo = sb("w_lo", [P, SKIPS, 2, G4], F32R, st)
            adjT_hi = sb("adjT_hi", [P, C, T], F32R, st)
            adjT_lo = sb("adjT_lo", [P, C, T], F32R, st)
            adjT = sb("adjT", [P, C, T], F32, st)
            wg0 = sb("wg0", [P, D], F32, st)
            wg0_hi = sb("wg0_hi", [P, D], F32R, st)
            wg0_lo = sb("wg0_lo", [P, D], F32R, st)
            wg1 = sb("wg1", [P, D], F32, st)
            bg0_rows = sb("bg0_rows", [P, D], F32, st)
            bg1_rows = sb("bg1_rows", [P, D], F32, st)
            bg0_adj = sb("bg0_adj", [P, T], F32, st)
            bias_nat = sb("bias_nat", [SKIPS * GATES, 2, P], F32, st)
            bias_sum = sb("bias_sum", [SKIPS * GATES, P], F32, st)
            bias = sb("bias", [P, SKIPS * GATES], F32, st)
            bias_half = sb("bias_half", [P, SKIPS * GATES], F32, st)
            x_hi = sb("x_hi", [P, 2, BU * C, D], F32R, st)
            x_lo = sb("x_lo", [P, 2, BU * C, D], F32R, st)
            ax_hi = sb("ax_hi", [P, 2, UNIT], F32R, st)
            ax_lo = sb("ax_lo", [P, 2, UNIT], F32R, st)
            h1b = sb("h1b", [P, 2, UNIT], F32, st)
            h1 = sb("h1", [P, 2, UNIT], F32, st)
            hw = sb("hw", [P, 2, BU * C, D], F32, st)
            hw_hi = sb("hw_hi", [P, 2, BU * C, D], F32R, st)
            hw_lo = sb("hw_lo", [P, 2, BU * C, D], F32R, st)
            gate = sb("gate", [P, 2, GATES, UNIT], F32, st)
            cell = sb("cell", [P, 2, UNIT], F32, st)
            hid = sb("hid", [P, 2, UNIT], F32, st)
            cell_t, incr, kept = h1b, h1, hw[:].rearrange("p s c d -> p s (c d)")
            hid_hi, hid_lo = ax_hi, ax_lo
            w_nat = gate[:].rearrange("p s g u -> p (s g u)").rearrange(
                "p (w l g k) -> p w l g k", w=2, l=SKIPS, g=GATES)

            bank = st.enter_context(nc.psum_tensor("bank", [P, 8, UNIT], F32))

            wih_loaded = sem("wih_loaded", st)
            whh_loaded = sem("whh_loaded", st)
            wg0_loaded = sem("wg0_loaded", st)
            wg1_loaded = sem("wg1_loaded", st)
            bg_loaded = sem("bg_loaded", st)
            bias_loaded = sem("bias_loaded", st)
            adj_t = sem("adj_t", st)
            adjT_made = sem("adjT_made", st)
            adjT_hi_made = sem("adjT_hi_made", st)
            wg0_made = sem("wg0_made", st)
            bias_summed = sem("bias_summed", st)
            bias_t = sem("bias_t", st)
            bias_made = sem("bias_made", st)
            bg0_ps = sem("bg0_ps", st)
            bg0_made = sem("bg0_made", st)
            w_t = sem("w_t", st)
            w_hi_made = sem("w_hi_made", st)
            w_lo_made = sem("w_lo_made", st)
            s_xh = sem("s_xh", st)
            s_xl = sem("s_xl", st)
            s_ax = sem("s_ax", st)
            s_axh = sem("s_axh", st)
            s_axl = sem("s_axl", st)
            s_h1p = sem("s_h1p", st)
            s_h1b = sem("s_h1b", st)
            s_h1 = sem("s_h1", st)
            s_hwp = sem("s_hwp", st)
            s_hw = sem("s_hw", st)
            s_hwh = sem("s_hwh", st)
            s_hwl = sem("s_hwl", st)
            s_h2p = sem("s_h2p", st)
            s_hh = sem("s_hh", st)
            s_hl = sem("s_hl", st)
            pre_done = [sem(f"pre_done{s}", st) for s in range(2)]
            gate_done = [sem(f"gate_done{s}", st) for s in range(2)]
            incr_done = [sem(f"incr_done{s}", st) for s in range(2)]
            kept_done = [sem(f"kept_done{s}", st) for s in range(2)]
            cell_done = [sem(f"cell_done{s}", st) for s in range(2)]
            tanh_done = [sem(f"tanh_done{s}", st) for s in range(2)]
            hid_done = [sem(f"hid_done{s}", st) for s in range(2)]
            hi_done = [sem(f"hi_done{s}", st) for s in range(2)]
            lo_done = [sem(f"lo_done{s}", st) for s in range(2)]

            LSTM_WEIGHTS = [(l, w) for l in range(SKIPS) for w in range(2) if (l, w) != (0, 1)]
            X_PARTS_AT = {0: [0], 4: [1, 2, 3]}

            PSUM_AX, PSUM_H1, PSUM_HW, PSUM_H2 = 0, 2, 4, 6

            BATCHES4 = 4
            UNITS_OF = {1: TOK // UNIT, 2: TOK // 2 // UNIT, 3: B // BATCHES4, 4: TOK // 4 // UNIT}
            WIN3 = T // 3
            N_OF = {1: UNIT, 2: UNIT, 3: BATCHES4 * WIN3, 4: UNIT}
            ITERS = {p: UNITS_OF[p] // 2 for p in UNITS_OF}
            GATES_OF = {p: 3 + 4 * (p - 1) for p in UNITS_OF}
            GATE_BASE = {p: sum(ITERS[q] * GATES_OF[q] for q in range(1, p)) for p in UNITS_OF}
            STEP_BASE = {p: sum(ITERS[q] * q for q in range(1, p)) for p in UNITS_OF}
            LATER_BASE = {p: sum(ITERS[q] * (q - 1) for q in range(1, p)) for p in UNITS_OF}
            ORDER0 = [2, 0, 3]
            ORDER = [2, 0, 1, 3]

            def tokens(h, p, unit, t):
                if p == 1:
                    return h[:, bass.ds(unit * UNIT, UNIT)]
                if p == 3:
                    v = h[:].rearrange("q (b t) -> q t b", t=T)
                    return v[:, t:t + 3 * (WIN3 - 1) + 1:3, bass.ds(unit * BATCHES4, BATCHES4)]
                v = h[:].rearrange("q (w t) -> q w t", t=p)
                return v[:, bass.ds(unit * UNIT, UNIT), t]

            def cut(ap, p):
                if p != 3:
                    return ap
                return ap[:, 0:N_OF[3]].rearrange("q (w b) -> q w b", b=BATCHES4)

            def gates_before(p, seq, t):
                return GATE_BASE[p] + seq * GATES_OF[p] + (0 if t == 0 else 3 + 4 * (t - 1))

            def steps_before(p, seq, t):
                return STEP_BASE[p] + seq * p + t

            def later_steps_before(p, seq, t):
                return LATER_BASE[p] + seq * (p - 1) + t - 1

            def graph_rounds(eng, graph_round):
                for r in range(3):
                    graph_round(r, r % 2)
                with eng.Fori(0, (UNITS - 6) // 2) as it:
                    graph_round(it * 2 + 3, 1)
                    graph_round(it * 2 + 4, 0)
                for r in range(UNITS - 3, UNITS + 1):
                    graph_round(r, r % 2)

            def lstm_steps(eng, start, finish):
                def first_lstm(seq, slot):
                    start(1, seq, slot, 0)
                    finish(1, seq if slot else seq - 1, 1 - slot, 0)

                start(1, 0, 0, 0)
                first_lstm(0, 1)
                first_lstm(1, 0)
                first_lstm(1, 1)
                with eng.Fori(1, ITERS[1] // 2) as it:
                    for k in range(2):
                        for slot in range(2):
                            first_lstm(it * 2 + k, slot)
                finish(1, ITERS[1] - 1, 1, 0)

                def unit_pair(p, seq, first):
                    for t in range(p):
                        for slot in range(2):
                            start(p, seq, slot, t)
                            if (slot, t) != (1, p - 1):
                                finish(p, seq, slot, t)
                            if (slot, t) == (0, 0) and not first:
                                finish(p, seq - 1, 1, p - 1)

                for p in range(2, SKIPS + 1):
                    unit_pair(p, 0, True)
                    with eng.Fori(1, ITERS[p]) as it:
                        unit_pair(p, it, False)
                    finish(p, ITERS[p] - 1, 1, p - 1)

            def there(n):
                return not isinstance(n, int) or 0 <= n < UNITS

            block = st.enter_context(nc.Block())

            @block.sync
            def _(sp):
                per = CH // len(x_loaded)
                sp.dma_start(adj_nat[:], adj.rearrange("(c p) s -> p c s", p=P)).then_inc(adj_loaded, 16)
                sp.dma_start(res[:, 0:per, :], x_v[:, 0:per, :]).then_inc(x_loaded[0], 16)
                for k in range(1, len(x_loaded)):
                    sp.dma_start(res[:, k * per:(k + 1) * per, :],
                                 x_v[:, k * per:(k + 1) * per, :]).then_inc(x_loaded[k], 16)
                sp.dma_start(w_nat[:, 0], Wih.rearrange("l (g r) k -> r l g k", r=P)).then_inc(wih_loaded, 16)
                sp.dma_start(w_nat[:, 1], Whh.rearrange("l (g r) k -> r l g k", r=P)).then_inc(whh_loaded, 16)
                sp.dma_start(wqkv[:], Wqkv).then_inc(wqkv_loaded, 16)
                sp.wait_ge(wqkv_loaded, 16)

            @block.gpsimd
            def _(pool):
                pool.memset(ident[:], 0.0).then_inc(ident_made, 1)
                pool.memset(head_rows[:], 1.0).then_inc(rows_made, 1)
                pool.wait_ge(ident_made, 1)
                pool.affine_select(out=ident[:], in_=ident[:], compare_op=ALU.not_equal, fill=1.0, base=0,
                                   pattern=[[-1, P]], channel_multiplier=1).then_inc(ident_made, 1)
                pool.wait_ge(rows_made, 1)
                pool.affine_select(out=head_rows[:], in_=head_rows[:], compare_op=ALU.is_ge, fill=0.0, base=0,
                                   pattern=[[-HD, HEADS]], channel_multiplier=1).then_inc(rows_made, 1)
                pool.wait_ge(rows_made, 2)
                pool.affine_select(out=head_rows[:], in_=head_rows[:], compare_op=ALU.is_ge, fill=0.0, base=HD - 1,
                                   pattern=[[HD, HEADS]], channel_multiplier=-1).then_inc(rows_made, 1)

                def split_x(n, slot):
                    if not there(n):
                        return
                    pool.wait_ge(s_xh, n + 1)
                    wait(pool, s_ax, n - 1)
                    pool.tensor_tensor(x_lo[:, slot], res[:, bass.ds(n * BU * C, BU * C), :],
                                       x_hi[:, slot].bitcast(F32), ALU.subtract).then_inc(s_xl, 1)

                def split_hw(n, slot):
                    if not there(n):
                        return
                    pool.wait_ge(s_hwh, n + 1)
                    wait(pool, s_h2p, n - 1)
                    pool.tensor_tensor(hw_lo[:, slot], hw[:, slot], hw_hi[:, slot].bitcast(F32),
                                       ALU.subtract).then_inc(s_hwl, 1)

                def graph_round(r, slot):
                    split_x(r + 2, slot)
                    split_hw(r, slot)

                split_x(0, 0)
                split_x(1, 1)
                graph_rounds(pool, graph_round)

                def low_part(p, seq, slot, t):
                    n = steps_before(p, seq, t)
                    unit = seq * 2 + slot
                    pool.wait_ge(hi_done[slot], n + 1)
                    full = cut(hid[:, slot], p)
                    if t == p - 1:
                        dst, hi = tokens(h_lo, p, unit, t), tokens(h_hi, p, unit, t)
                    else:
                        dst, hi = cut(hid_lo[:, slot], p), cut(hid_hi[:, slot], p)
                    pool.tensor_tensor(dst, full, hi.bitcast(F32), ALU.subtract).then_inc(lo_done[slot], 1)

                lstm_steps(pool, lambda *step: None, low_part)

            @block.scalar
            def _(act):
                act.dma_start(wg0[:], Wg0).then_inc(wg0_loaded, 16)
                act.dma_start(bg0_rows[:], bg0.partition_broadcast(P)).then_inc(bg_loaded, 16)
                act.dma_start(wg1[:], Wg1).then_inc(wg1_loaded, 16)
                act.dma_start(bg1_rows[:], bg1.partition_broadcast(P)).then_inc(bg_loaded, 16)
                act.dma_start(bias_nat[:, 0, :], bih.rearrange("l (g r) -> (l g) r", r=P)).then_inc(bias_loaded, 16)
                act.dma_start(bias_nat[:, 1, :], bhh.rearrange("l (g r) -> (l g) r", r=P)).then_inc(bias_loaded, 16)

                def round_x(n, slot):
                    if not there(n):
                        return
                    if isinstance(n, int) and n in X_PARTS_AT:
                        for k in X_PARTS_AT[n]:
                            act.wait_ge(x_loaded[k], 16)
                    wait(act, s_ax, n - 1)
                    wait(act, s_xl, n - 1)
                    act.activation(x_hi[:, slot], res[:, bass.ds(n * BU * C, BU * C), :],
                                   ACT.Copy).then_inc(s_xh, 1)

                def graph_round(r, slot):
                    nxt = 1 - slot
                    if there(r + 1):
                        n = r + 1
                        act.wait_ge(s_ax, n + 1)
                        wait(act, s_h1p, n - 1)
                        wait(act, s_axl, n - 1)
                        act.activation(ax_hi[:, nxt], bank[:, PSUM_AX + nxt, :], ACT.Copy).then_inc(s_axh, 1)
                    round_x(r + 2, slot)
                    if there(r):
                        act.wait_ge(s_hw, r + 1)
                        wait(act, s_h2p, r - 1)
                        wait(act, s_hwl, r - 1)
                        act.activation(hw_hi[:, slot], hw[:, slot], ACT.Copy).then_inc(s_hwh, 1)
                    if there(r - 1):
                        n = r - 1
                        act.wait_ge(s_h2p, n + 1)
                        act.activation(h_hi[:, bass.ds(n * UNIT, UNIT)], bank[:, PSUM_H2 + nxt, :],
                                       ACT.Relu).then_inc(s_hh, 1)
                    if there(r + 1):
                        n = r + 1
                        act.wait_ge(s_h1b, n + 1)
                        wait(act, s_hwp, n - 1)
                        act.activation(h1[:, nxt], h1b[:, nxt], ACT.Relu).then_inc(s_h1, 1)

                act.wait_ge(adjT_made, 1)
                act.activation(adjT_hi[:].rearrange("p c t -> p (c t)"), bank[:, 7, :],
                               ACT.Copy).then_inc(adjT_hi_made, 1)
                round_x(0, 0)
                graph_round(-1, 1)
                graph_rounds(act, graph_round)

                for k, (l, w) in enumerate(LSTM_WEIGHTS):
                    act.wait_ge(w_t, k + 1)
                    act.activation(w_hi[:, l, w, :], bank[:, k % 6, :], ACT.Copy,
                                   scale=1.0 if k == 0 else 0.5).then_inc(w_hi_made, 1)

                act.wait_ge(bias_made, 2)

                def gates(p, seq, slot, t):
                    g0, n = gates_before(p, seq, t), steps_before(p, seq, t)
                    for k, g in enumerate(ORDER if t else ORDER0):
                        act.wait_ge(pre_done[slot], g0 + k + 1)
                        if g == 3:
                            wait(act, hid_done[slot], n)
                        b = (bias if g == 2 else bias_half)[:, (p - 1) * GATES + g:(p - 1) * GATES + g + 1]
                        act.activation(gate[:, slot, g, 0:N_OF[p]], bank[:, slot * GATES + g, 0:N_OF[p]], ACT.Tanh,
                                       bias=b, scale=1.0 if g == 2 else 0.5).then_inc(gate_done[slot], 1)

                def cell_tanh(p, seq, slot, t):
                    n = steps_before(p, seq, t)
                    act.wait_ge(cell_done[slot], n + 1)
                    act.activation(cell_t[:, slot, 0:N_OF[p]], cell[:, slot, 0:N_OF[p]], ACT.Tanh,
                                   scale=0.5).then_inc(tanh_done[slot], 1)

                lstm_steps(act, gates, cell_tanh)

            @block.vector
            def _(dve):
                dve.wait_ge(adj_loaded, 16)
                dve.tensor_scalar(mask[:], adj_nat[:], 0.0, MASKED, ALU.is_equal, ALU.mult).then_inc(mask_made, 1)
                dve.wait_ge(ident_made, 2)
                dve.tensor_copy(ident_bf[:], ident[:]).then_inc(ident_bf_made, 1)
                dve.wait_ge(adj_t, 1)
                flat = adjT[:].rearrange("p c t -> p (c t)")
                dve.tensor_copy(flat, bank[:, 7, :]).then_inc(adjT_made, 1)
                dve.wait_ge(adjT_made, 1)
                dve.wait_ge(adjT_hi_made, 1)
                dve.tensor_tensor(adjT_lo[:], adjT[:], adjT_hi[:].bitcast(F32), ALU.subtract).then_inc(adjT_made, 1)
                dve.wait_ge(wg0_loaded, 16)
                dve.tensor_copy(wg0_hi[:], wg0[:]).then_inc(wg0_made, 1)
                dve.wait_ge(wg0_made, 1)
                dve.tensor_tensor(wg0_lo[:], wg0[:], wg0_hi[:].bitcast(F32), ALU.subtract).then_inc(wg0_made, 1)
                bg0_b = bg0_adj[:].unsqueeze(1).broadcast_to([P, BU, T])
                bg1_b = bg1_rows[:].unsqueeze(1).broadcast_to([P, BU * C, D])

                def graph_round(r, slot):
                    nxt = 1 - slot
                    if there(r + 1):
                        n = r + 1
                        dve.wait_ge(s_axh, n + 1)
                        wait(dve, s_h1p, n - 1)
                        dve.tensor_tensor(ax_lo[:, nxt], bank[:, PSUM_AX + nxt, :], ax_hi[:, nxt].bitcast(F32),
                                          ALU.subtract).then_inc(s_axl, 1)
                    if there(r):
                        dve.wait_ge(s_hwp, r + 1)
                        wait(dve, s_hwh, r - 1)
                        wait(dve, s_hwl, r - 1)
                        dve.tensor_tensor(hw[:, slot], bank[:, PSUM_HW + slot, :].rearrange("p (c d) -> p c d", d=D),
                                          bg1_b, ALU.add).then_inc(s_hw, 1)
                    if isinstance(r, int) and r == -1:
                        dve.wait_ge(bg0_ps, 1)
                        dve.tensor_copy(bg0_adj[:], bank[:, 7, 0:T]).then_inc(bg0_made, 1)
                        dve.wait_ge(bg0_made, 1)
                        dve.wait_ge(bg_loaded, 32)
                    if there(r + 1):
                        n = r + 1
                        dve.wait_ge(s_h1p, n + 1)
                        wait(dve, s_h1, n - 1)
                        dve.tensor_tensor(h1b[:, nxt].rearrange("p (b t) -> p b t", t=T),
                                          bank[:, PSUM_H1 + nxt, :].rearrange("p (b t) -> p b t", t=T),
                                          bg0_b, ALU.add).then_inc(s_h1b, 1)
                    if there(r - 1):
                        n = r - 1
                        dve.wait_ge(s_hh, n + 1)
                        dve.scalar_tensor_tensor(h_lo[:, bass.ds(n * UNIT, UNIT)], bank[:, PSUM_H2 + nxt, :], 0.0,
                                                 h_hi[:, bass.ds(n * UNIT, UNIT)].bitcast(F32), ALU.max,
                                                 ALU.subtract).then_inc(s_hl, 1)

                graph_round(-1, 1)
                graph_rounds(dve, graph_round)
                for k, (l, w) in enumerate(LSTM_WEIGHTS):
                    dve.wait_ge(w_hi_made, k + 1)
                    dve.scalar_tensor_tensor(w_lo[:, l, w, :], bank[:, k % 6, :], 1.0 if k == 0 else 0.5,
                                             w_hi[:, l, w, :].bitcast(F32), ALU.mult,
                                             ALU.subtract).then_inc(w_lo_made, 1)
                dve.wait_ge(bias_loaded, 32)
                dve.tensor_tensor(bias_sum[:], bias_nat[:, 0, :], bias_nat[:, 1, :], ALU.add).then_inc(bias_summed, 1)
                dve.wait_ge(bias_t, 1)
                dve.tensor_copy(bias[:], bank[:, 6, 0:SKIPS * GATES]).then_inc(bias_made, 1)
                dve.tensor_scalar(bias_half[:], bank[:, 6, 0:SKIPS * GATES], 0.5, None, ALU.mult).then_inc(bias_made, 1)

                def cell_state(p, seq, slot, t):
                    g0, n = gates_before(p, seq, t), steps_before(p, seq, t)
                    w = slice(0, N_OF[p])
                    g_i, g_f, g_g = (gate[:, slot, g, w] for g in range(3))
                    dve.wait_ge(gate_done[slot], g0 + 2)
                    if t == 0:
                        wait(dve, tanh_done[slot], n)
                        dve.scalar_tensor_tensor(cell[:, slot, w], g_i, 1.0, g_g, ALU.add,
                                                 ALU.mult).then_inc(cell_done[slot], 1)
                    else:
                        m = later_steps_before(p, seq, t)
                        dve.scalar_tensor_tensor(incr[:, slot, w], g_i, 1.0, g_g, ALU.add,
                                                 ALU.mult).then_inc(incr_done[slot], 1)
                        dve.wait_ge(gate_done[slot], g0 + 3)
                        dve.scalar_tensor_tensor(kept[:, slot, w], g_f, 1.0, cell[:, slot, w], ALU.add,
                                                 ALU.mult).then_inc(kept_done[slot], 1)
                        dve.wait_ge(incr_done[slot], m + 1)
                        dve.wait_ge(kept_done[slot], m + 1)
                        dve.scalar_tensor_tensor(cell[:, slot, w], kept[:, slot, w], 0.5, incr[:, slot, w], ALU.mult,
                                                 ALU.add).then_inc(cell_done[slot], 1)

                def hidden_state(p, seq, slot, t):
                    n = steps_before(p, seq, t)
                    unit = seq * 2 + slot
                    w = slice(0, N_OF[p])
                    dve.wait_ge(gate_done[slot], gates_before(p, seq, t) + (4 if t else 3))
                    dve.wait_ge(tanh_done[slot], n + 1)
                    wait(dve, lo_done[slot], n)
                    dve.scalar_tensor_tensor(hid[:, slot, w], gate[:, slot, 3, w], 1.0, cell_t[:, slot, w], ALU.add,
                                             ALU.mult).then_inc(hid_done[slot], 1)
                    dve.wait_ge(hid_done[slot], n + 1)
                    dst = tokens(h_hi, p, unit, t) if t == p - 1 else cut(hid_hi[:, slot], p)
                    dve.tensor_copy(dst, cut(hid[:, slot], p)).then_inc(hi_done[slot], 1)

                lstm_steps(dve, cell_state, hidden_state)

            @block.tensor
            def _(pe):
                def product3(out_ap, lhs_hi, lhs_lo, rhs_hi, rhs_lo, start=True, stop=True):
                    pe.matmul(out_ap, lhs_hi, rhs_hi, start=start, stop=False)
                    pe.matmul(out_ap, lhs_hi, rhs_lo, start=False, stop=False)
                    return pe.matmul(out_ap, lhs_lo, rhs_hi, start=False, stop=stop)

                pe.wait_ge(adj_loaded, 16)
                pe.wait_ge(ident_made, 2)
                for s in range(C):
                    for t in range(C):
                        last = pe.transpose(bank[:, 7, s * T + t * P:s * T + (t + 1) * P],
                                            adj_nat[:, t, s * P:(s + 1) * P], ident[:])
                last.then_inc(adj_t, 1)
                pe.wait_ge(adjT_made, 2)

                def adj_x(n, slot):
                    pe.wait_ge(s_xh, n + 1)
                    pe.wait_ge(s_xl, n + 1)
                    wait(pe, s_axl, n - 1)
                    for b in range(BU):
                        o = bank[:, PSUM_AX + slot, b * T:(b + 1) * T]
                        for s in range(C):
                            last = product3(o, x_hi[:, slot, b * C + s, :], x_lo[:, slot, b * C + s, :],
                                            adjT_hi[:, s, :], adjT_lo[:, s, :], s == 0, s == C - 1)
                    last.then_inc(s_ax, 1)

                def layer1(n, slot):
                    pe.wait_ge(s_axh, n + 1)
                    pe.wait_ge(s_axl, n + 1)
                    wait(pe, s_h1b, n - 1)
                    product3(bank[:, PSUM_H1 + slot, :], wg0_hi[:], wg0_lo[:], ax_hi[:, slot],
                             ax_lo[:, slot]).then_inc(s_h1p, 1)

                def weight2(n, slot):
                    pe.wait_ge(s_h1, n + 1)
                    wait(pe, s_hw, n - 1)
                    for c in range(BU * C):
                        last = pe.matmul(bank[:, PSUM_HW + slot, c * D:(c + 1) * D], h1[:, slot, c * P:(c + 1) * P],
                                         wg1[:], start=True, stop=True)
                    last.then_inc(s_hwp, 1)

                def layer2(n, slot):
                    pe.wait_ge(s_hwh, n + 1)
                    pe.wait_ge(s_hwl, n + 1)
                    wait(pe, s_hl, n - 1)
                    for b in range(BU):
                        o = bank[:, PSUM_H2 + slot, b * T:(b + 1) * T]
                        for s in range(C):
                            last = product3(o, hw_hi[:, slot, b * C + s, :], hw_lo[:, slot, b * C + s, :],
                                            adjT_hi[:, s, :], adjT_lo[:, s, :], s == 0, s == C - 1)
                    last.then_inc(s_h2p, 1)

                def graph_round(r, slot):
                    nxt = 1 - slot
                    if there(r + 1):
                        adj_x(r + 1, nxt)
                    if there(r):
                        weight2(r, slot)
                    if there(r - 1):
                        layer2(r - 1, nxt)
                    if there(r + 1):
                        layer1(r + 1, nxt)

                adj_x(0, 0)
                pe.wait_ge(wg0_made, 2)
                layer1(0, 0)
                pe.wait_ge(bg_loaded, 32)
                for s in range(C):
                    last = pe.matmul(bank[:, 7, 0:T], bg0_rows[:], adjT[:, s, :], start=(s == 0), stop=(s == C - 1))
                last.then_inc(bg0_ps, 1)
                pe.wait_ge(bg0_made, 1)
                pe.wait_ge(wg1_loaded, 16)
                graph_rounds(pe, graph_round)
                pe.wait_ge(s_axl, UNITS)
                pe.wait_ge(s_h1b, UNITS)
                pe.wait_ge(s_hw, UNITS)
                pe.wait_ge(wih_loaded, 16)
                pe.wait_ge(whh_loaded, 16)
                for k, (l, w) in enumerate(LSTM_WEIGHTS):
                    if k >= 6:
                        pe.wait_ge(w_lo_made, k - 5)
                    for g in range(GATES):
                        last = pe.transpose(bank[:, k % 6, g * P:(g + 1) * P], w_nat[:, w, l, g, :], ident[:])
                    last.then_inc(w_t, 1)
                pe.wait_ge(s_hh, UNITS)
                pe.wait_ge(s_hl, UNITS)
                pe.wait_ge(bias_summed, 1)
                n_b = SKIPS * GATES
                pe.transpose(bank[:, 6, 0:n_b], bias_sum[:], ident[0:n_b, 0:n_b]).then_inc(bias_t, 1)
                pe.wait_ge(w_lo_made, len(LSTM_WEIGHTS))
                pe.wait_ge(bias_made, 2)

                def gate_products(p, seq, slot, t):
                    g0, n = gates_before(p, seq, t), steps_before(p, seq, t)
                    unit = seq * 2 + slot
                    order = ORDER if t else ORDER0
                    if t == 0 and p == 2:
                        for s in range(2):
                            pe.wait_ge(hi_done[s], STEP_BASE[1] + unit + 1)
                            pe.wait_ge(lo_done[s], STEP_BASE[1] + unit + 1)
                    if t == 0 and p == 3:
                        pe.wait_ge(hi_done[slot], STEP_BASE[2] + (seq + 1) * 2)
                        pe.wait_ge(lo_done[slot], STEP_BASE[2] + (seq + 1) * 2)
                    if t == 0 and p == 4:
                        for s in range(2):
                            pe.wait_ge(hi_done[s], STEP_BASE[3] + (unit + 1) * 3)
                            pe.wait_ge(lo_done[s], STEP_BASE[3] + (unit + 1) * 3)
                    wait(pe, gate_done[slot], g0)
                    x_h, x_l = tokens(h_hi, p, unit, t), tokens(h_lo, p, unit, t)
                    for g in order:
                        cols = slice(g * P, (g + 1) * P)
                        last = product3(cut(bank[:, slot * GATES + g], p), w_hi[:, p - 1, 0, cols],
                                        w_lo[:, p - 1, 0, cols], x_h, x_l, True, t == 0)
                        if t == 0:
                            last.then_inc(pre_done[slot], 1)
                    if t > 0:
                        pe.wait_ge(hi_done[slot], n)
                        pe.wait_ge(lo_done[slot], n)
                        for g in order:
                            cols = slice(g * P, (g + 1) * P)
                            product3(cut(bank[:, slot * GATES + g], p), w_hi[:, p - 1, 1, cols],
                                     w_lo[:, p - 1, 1, cols], cut(hid_hi[:, slot], p), cut(hid_lo[:, slot], p),
                                     False, True).then_inc(pre_done[slot], 1)

                lstm_steps(pe, gate_products, lambda *step: None)

        with ExitStack() as st:
            hsum = sb("hsum", [P, 2, T], F32, st)
            stats = sb("stats", [P, 2, 2 * C, 6], F32, st)
            moments = sb("moments", [P, 2, 2 * C, 2], F32, st)
            eps_col = sb("eps_col", [P, 1], F32, st)
            log_var = sb("log_var", [P, 2 * C], F32, st)
            root = sb("root", [P, 2 * C], F32, st)
            root_sq = sb("root_sq", [P, 2 * C], F32, st)
            root_err = sb("root_err", [P, 2 * C], F32, st)
            root_fix = sb("root_fix", [P, 2 * C], F32, st)
            rstd = sb("rstd", [P, 2, 2 * C], F32, st)
            centred = sb("centred", [P, 2, C, D], F32, st)
            result = sb("result", [P, 2, C, D], F32, st)
            y_in = sb("y_in", [P, 2, C, D], F32, st)
            yT = sb("yT", [P, 2, T], F32, st)
            qk_hi = sb("qk_hi", [P, 2, 2 * T], F32R, st)
            qk_lo = sb("qk_lo", [P, 2, 2 * T], F32R, st)
            kp_hi = sb("kp_hi", [P, 2, HEADS, T], F32R, st)
            kp_lo = sb("kp_lo", [P, 2, HEADS, T], F32R, st)
            v = sb("v", [P, 2, C, D], F32, st)
            neg_max = sb("neg_max", [P, 2, C * HEADS], F32, st)
            exp_bias = sb("exp_bias", [P, 2, C * HEADS], F32, st)
            prob = sb("prob", [P, 2, C, HEADS, T], F32, st)
            prob_sum = sb("prob_sum", [P, 2, C * HEADS], F32, st)
            inv_sum = sb("inv_sum", [P, 2, C * HEADS], F32, st)
            probT = sb("probT", [P, HEADS, C, T], F32, st)
            oT = sb("oT", [P, T], F32, st)
            attn = sb("attn", [P, 2, C, D], F32, st)

            bank = st.enter_context(nc.psum_tensor("bank2", [P, 8, UNIT], F32))
            SCORE_BANKS = [(0, 0), (1, 0), (0, 1), (1, 1)]
            PSUM_PT, PSUM_QKV, PSUM_O = 4, 6, 7

            s_hsum = sem("s_hsum", st)
            s_hT = sem("s_hT", st)
            s_y = sem("s_y", st)
            y_stats = sem("y_stats", st)
            y_normed = sem("y_normed", st)
            sum_made = sem("sum_made", st)
            sum_stats = sem("sum_stats", st)
            out_centred = sem("out_centred", st)
            out_normed = sem("out_normed", st)
            out_written = [sem(f"out_written{s}", st) for s in range(2)]
            eps_set = sem("eps_set", st)
            moments_made = sem("moments_made", st)
            log_made = sem("log_made", st)
            root_made = sem("root_made", st)
            root_sq_made = sem("root_sq_made", st)
            root_err_made = sem("root_err_made", st)
            root_fix_made = sem("root_fix_made", st)
            rstd_made = sem("rstd_made", st)
            y_staged = [sem(f"y_staged{s}", st) for s in range(2)]
            s_yT = sem("s_yT", st)
            yT_made = sem("yT_made", st)
            s_qk = sem("s_qk", st)
            qk_hi_made = sem("qk_hi_made", st)
            qk_lo_made = sem("qk_lo_made", st)
            kp_made = sem("kp_made", st)
            s_v = sem("s_v", st)
            v_made = sem("v_made", st)
            s_scores = sem("s_scores", st)
            max_made = sem("max_made", st)
            bias_ready = sem("bias_ready", st)
            exp_done = sem("exp_done", st)
            s_probT = sem("s_probT", st)
            probT_dve = sem("probT_dve", st)
            probT_act = sem("probT_act", st)
            s_o = sem("s_o", st)
            oT_made = sem("oT_made", st)
            s_oT = sem("s_oT", st)
            inv_made = sem("inv_made", st)
            attn_made = sem("attn_made", st)

            PAIR = HEADS // 2

            LEAD = 5
            SUM_LAG = 3
            OUT_LAG = 4
            LOOP_FROM, LOOP_TO = OUT_LAG + 3, B - LEAD

            def batch_rounds(eng, batch_round):
                for r in range(-LEAD, LOOP_FROM):
                    batch_round(r, r % 2)
                with eng.Fori(0, (LOOP_TO - LOOP_FROM) // 2) as it:
                    batch_round(it * 2 + LOOP_FROM, 1)
                    batch_round(it * 2 + LOOP_FROM + 1, 0)
                for r in range(LOOP_TO, B + OUT_LAG):
                    batch_round(r, r % 2)

            def here(n):
                return not isinstance(n, int) or 0 <= n < B

            def wait_apart(eng, *pairs):
                eng.wait_ge(ident_made, 2)
                for semaphore, value in pairs:
                    wait(eng, semaphore, value)

            def tokens_of(n):
                return res[:, bass.ds(n * C, C), :]

            def moment_columns(r):
                return slice(0 if here(r + LEAD - 1) else C, 2 * C if here(r - SUM_LAG) else C)

            def moment_rounds(r):
                return r + LEAD if not isinstance(r, int) or r < B + SUM_LAG else 0

            def some(count):
                return not isinstance(count, int) or count > 0

            block = st.enter_context(nc.Block())

            @block.sync
            def _(sp):
                def batch_round(r, slot):
                    if here(r + LEAD - 2):
                        n = r + LEAD - 2
                        if isinstance(r, int):
                            wait(sp, s_yT, n - 1)
                        sp.wait_ge(y_normed, n + 1)
                        sp.dma_start(y_in[:, 1 - slot], tokens_of(n)).then_inc(y_staged[1 - slot], 16)
                    if here(r - OUT_LAG):
                        n = r - OUT_LAG
                        sp.wait_ge(out_normed, n + 1)
                        sp.dma_start(out_v[:, bass.ds(n * C, C), :], result[:, slot]).then_inc(out_written[slot], 16)

                batch_rounds(sp, batch_round)
                for slot in range(2):
                    sp.wait_ge(out_written[slot], 16 * B // 2)

            @block.gpsimd
            def _(pool):
                pool.memset(eps_col[:], EPS).then_inc(eps_set, 1)

                def head_keys(n, slot, pair):
                    heads = slice(pair * PAIR, (pair + 1) * PAIR)
                    rows = head_rows[:, heads].unsqueeze(2).broadcast_to([P, PAIR, T])
                    for part, made, dst in ((qk_hi, qk_hi_made, kp_hi), (qk_lo, qk_lo_made, kp_lo)):
                        pool.wait_ge(made, n + 1)
                        if pair == 0:
                            wait(pool, s_scores, (n - 1) * 4)
                        k_b = part[:, slot, T:2 * T].bitcast(F32).unsqueeze(1).broadcast_to([P, PAIR, T])
                        pool.tensor_tensor(dst[:, slot, heads, :], k_b, rows, ALU.mult).then_inc(kp_made, 1)

                def batch_round(r, slot):
                    nxt = 1 - slot
                    if here(r + LEAD):
                        n = r + LEAD
                        wait_apart(pool, (s_hT, n - 1))
                        pool.tensor_tensor(hsum[:, nxt], h_hi[:, bass.ds(n * T, T)].bitcast(F32),
                                           h_lo[:, bass.ds(n * T, T)].bitcast(F32), ALU.add).then_inc(s_hsum, 1)
                    if here(r + 1):
                        head_keys(r + 1, nxt, 0)
                    if here(r - 2):
                        n = r - 2
                        wait_apart(pool, (attn_made, n + 1))
                        pool.tensor_tensor(tokens_of(n), tokens_of(n), attn[:, slot], ALU.add).then_inc(sum_made, 1)
                    if here(r + 1):
                        head_keys(r + 1, nxt, 1)
                    if here(r - OUT_LAG):
                        n = r - OUT_LAG
                        mean = moments[:, nxt, C:2 * C, 0].unsqueeze(2).broadcast_to([P, C, D])
                        scale = rstd[:, slot, C:2 * C].unsqueeze(2).broadcast_to([P, C, D])
                        wait_apart(pool, (rstd_made, moment_rounds(r - 1)))
                        pool.tensor_tensor(centred[:, slot], tokens_of(n), mean, ALU.subtract).then_inc(out_centred, 1)
                        pool.wait_ge(out_centred, n + 1)
                        if here(n - 2):
                            pool.wait_ge(out_written[slot], 8 * n - (8 if slot else 0))
                        pool.tensor_tensor(result[:, slot], centred[:, slot], scale, ALU.mult).then_inc(out_normed, 1)

                batch_rounds(pool, batch_round)

            @block.scalar
            def _(act):
                act.preload_act_table_set("natural_log_exp_and_others")
                act.wait_ge(eps_set, 1)

                def scores_exp(r, slot, k):
                    if here(r):
                        c, pair = SCORE_BANKS[k]
                        if k == 0:
                            wait(act, s_probT, (r - 1) * 4)
                            wait(act, inv_made, r - 1)
                        act.wait_ge(bias_ready, r * 4 + k + 1)
                        for j in range(PAIR):
                            h = pair * PAIR + j
                            col = c * HEADS + h
                            ins = act.activation(prob[:, slot, c, h, :], bank[:, k, j * T:(j + 1) * T], ACT.Exp,
                                                 bias=exp_bias[:, slot, col:col + 1], scale=SCALE,
                                                 accum_out=prob_sum[:, slot, col:col + 1])
                        ins.then_inc(exp_done, 1)

                def batch_round(r, slot):
                    nxt = 1 - slot
                    if here(r + 1):
                        act.wait_ge(s_yT, r + 2)
                        wait(act, s_v, r)
                        act.activation(yT[:, nxt], bank[:, PSUM_QKV, 0:T], ACT.Copy).then_inc(yT_made, 1)
                    if here(r - 2):
                        act.wait_ge(s_o, r - 1)
                        wait(act, s_oT, r - 2)
                        act.activation(oT[:], bank[:, PSUM_O, 0:T], ACT.Copy).then_inc(oT_made, 1)
                    scores_exp(r - 1, nxt, 3)
                    k, cols = moment_rounds(r - 1), moment_columns(r - 1)
                    if some(k):
                        act.wait_ge(moments_made, k)
                        wait(act, root_made, k - 1)
                        act.activation(log_var[:, cols], moments[:, nxt, cols, 1], ACT.Ln,
                                       bias=eps_col[:]).then_inc(log_made, 1)
                        act.wait_ge(log_made, k)
                        wait(act, rstd_made, k - 1)
                        act.activation(root[:, cols], log_var[:, cols], ACT.Exp, scale=-0.5).then_inc(root_made, 1)
                    if here(r + 1):
                        act.wait_ge(s_qk, r + 2)
                        wait(act, s_scores, r * 4)
                        wait(act, kp_made, r * 4)
                        act.activation(qk_hi[:, nxt], bank[:, PSUM_QKV, :], ACT.Copy).then_inc(qk_hi_made, 1)
                    scores_exp(r, slot, 0)
                    if here(r - 1):
                        for h in range(2, HEADS):
                            act.wait_ge(s_probT, (r - 1) * 4 + h + 1)
                            wait(act, s_o, r - 1)
                            act.activation(probT[:, h].rearrange("p c t -> p (c t)"), bank[:, PSUM_PT + h % 2, :],
                                           ACT.Copy).then_inc(probT_act, 1)
                    if here(r):
                        act.wait_ge(s_v, r + 1)
                        wait(act, s_o, r - 1)
                        act.activation(v[:, slot].rearrange("p c d -> p (c d)"), bank[:, PSUM_QKV, 0:C * D],
                                       ACT.Copy).then_inc(v_made, 1)
                    scores_exp(r, slot, 1)
                    scores_exp(r, slot, 2)

                batch_rounds(act, batch_round)

            @block.vector
            def _(dve):
                def row_max(r, slot, k):
                    if here(r):
                        c, pair = SCORE_BANKS[k]
                        cols = slice(c * HEADS + pair * PAIR, c * HEADS + (pair + 1) * PAIR)
                        dve.wait_ge(s_scores, r * 4 + k + 1)
                        wait(dve, exp_done, (r - 1) * 4)
                        dve.tensor_reduce(neg_max[:, slot, cols], bank[:, k, :].rearrange("p (h t) -> p h t", t=T),
                                          AX.X, ALU.max, negate=True).then_inc(max_made, 1)
                        dve.wait_ge(max_made, r * 4 + k + 1)
                        dve.tensor_scalar(exp_bias[:, slot, cols], neg_max[:, slot, cols], SCALE, None,
                                          ALU.mult).then_inc(bias_ready, 1)

                def batch_round(r, slot):
                    nxt = 1 - slot
                    if here(r - 1):
                        for h in range(2):
                            dve.wait_ge(s_probT, (r - 1) * 4 + h + 1)
                            wait(dve, s_o, r - 1)
                            dve.tensor_copy(probT[:, h].rearrange("p c t -> p (c t)"),
                                            bank[:, PSUM_PT + h % 2, :]).then_inc(probT_dve, 1)
                    row_max(r, slot, 0)
                    if here(r - 2):
                        dve.wait_ge(exp_done, (r - 1) * 4)
                        dve.reciprocal(inv_sum[:, slot], prob_sum[:, slot]).then_inc(inv_made, 1)
                    k, cols = moment_rounds(r - 1), moment_columns(r - 1)
                    if some(k):
                        dve.wait_ge(root_made, k)
                        dve.tensor_tensor(root_sq[:, cols], root[:, cols], root[:, cols],
                                          ALU.mult).then_inc(root_sq_made, 1)
                    if here(r + 1):
                        dve.wait_ge(qk_hi_made, r + 2)
                        wait(dve, s_scores, r * 4)
                        wait(dve, kp_made, r * 4)
                        dve.tensor_tensor(qk_lo[:, nxt], bank[:, PSUM_QKV, :], qk_hi[:, nxt].bitcast(F32),
                                          ALU.subtract).then_inc(qk_lo_made, 1)
                    if some(k):
                        dve.wait_ge(root_sq_made, k)
                        dve.scalar_tensor_tensor(root_err[:, cols], moments[:, nxt, cols, 1], EPS, root_sq[:, cols],
                                                 ALU.add, ALU.mult).then_inc(root_err_made, 1)
                    if here(r - 2):
                        dve.wait_ge(s_oT, r - 1)
                        dve.wait_ge(inv_made, r - 1)
                        wait(dve, sum_made, r - 3)
                        dve.tensor_tensor(attn[:, slot].rearrange("p c (h d) -> p (c h) d", d=HD),
                                          bank[:, PSUM_O, T:2 * T].rearrange("p (g d) -> p g d", d=HD),
                                          inv_sum[:, slot].unsqueeze(2).broadcast_to([P, C * HEADS, HD]),
                                          ALU.mult).then_inc(attn_made, 1)
                    if some(k):
                        dve.wait_ge(root_err_made, k)
                        dve.tensor_scalar(root_fix[:, cols], root_err[:, cols], -0.5, 1.5, ALU.mult,
                                          ALU.add).then_inc(root_fix_made, 1)
                    row_max(r, slot, 1)
                    if some(k):
                        dve.wait_ge(root_fix_made, k)
                        wait(dve, out_normed, r - OUT_LAG - 1)
                        dve.tensor_tensor(rstd[:, slot, cols], root_fix[:, cols], root[:, cols],
                                          ALU.mult).then_inc(rstd_made, 1)
                    if here(r + LEAD - 1):
                        n = r + LEAD - 1
                        wait_apart(dve, (s_y, n + 1))
                        for c in range(C):
                            ins = dve.bn_stats(stats[:, slot, c, :], res[:, bass.ds(n * C + c, 1), :])
                        ins.then_inc(y_stats, 1)
                    if here(r + LEAD - 2):
                        n = r + LEAD - 2
                        wait_apart(dve, (rstd_made, k))
                        for c in range(C):
                            ap = res[:, bass.ds(n * C + c, 1), :]
                            ins = dve.tensor_scalar(ap, ap, moments[:, nxt, c, 0:1], rstd[:, slot, c:c + 1],
                                                    ALU.subtract, ALU.mult)
                        ins.then_inc(y_normed, 1)
                    if here(r - SUM_LAG):
                        n = r - SUM_LAG
                        wait_apart(dve, (sum_made, n + 1), (out_centred, r - OUT_LAG))
                        for c in range(C):
                            ins = dve.bn_stats(stats[:, slot, C + c, :], res[:, bass.ds(n * C + c, 1), :])
                        ins.then_inc(sum_stats, 1)
                    if here(r + LEAD):
                        n = r + LEAD
                        dve.wait_ge(s_hT, n + 1)
                        if here(r):
                            dve.wait_ge(v_made, r + 1)
                        dve.scalar_tensor_tensor(tokens_of(n), bank[:, PSUM_QKV, T:2 * T].rearrange(
                            "p (c d) -> p c d", d=D), 0.5, tokens_of(n), ALU.mult, ALU.add).then_inc(s_y, 1)
                    row_max(r, slot, 2)
                    if some(moment_rounds(r)):
                        waits = []
                        if here(r + LEAD - 1):
                            waits.append((y_stats, r + LEAD))
                        if here(r - SUM_LAG):
                            waits.append((sum_stats, r - SUM_LAG + 1))
                        wait_apart(dve, *waits)
                        cols = moment_columns(r)
                        for c in range(cols.start, cols.stop):
                            ins = dve.bn_aggr(moments[:, slot, c, :], stats[:, slot, c, :])
                        ins.then_inc(moments_made, 1)
                    row_max(r, slot, 3)

                batch_rounds(dve, batch_round)

            @block.tensor
            def _(pe):
                def scores(r, slot, k):
                    if here(r):
                        c, pair = SCORE_BANKS[k]
                        heads = slice(pair * PAIR, (pair + 1) * PAIR)
                        wait(pe, exp_done, (r - 1) * 4 + k + 1)
                        pe.matmul(bank[:, k, :], ident_bf[:], mask[:, c, :].unsqueeze(1).broadcast_to([P, PAIR, T]),
                                  start=True, stop=False)
                        pe.wait_ge(qk_lo_made, r + 1)
                        pe.wait_ge(kp_made, r * 4 + 2 * pair + 2)
                        q_hi = qk_hi[:, slot, c * P:(c + 1) * P]
                        q_lo = qk_lo[:, slot, c * P:(c + 1) * P]
                        k_hi, k_lo = (a[:, slot, heads, :].rearrange("p h t -> p (h t)") for a in (kp_hi, kp_lo))
                        pe.matmul(bank[:, k, :], q_hi, k_hi, start=False, stop=False)
                        pe.matmul(bank[:, k, :], q_hi, k_lo, start=False, stop=False)
                        pe.matmul(bank[:, k, :], q_lo, k_hi, start=False, stop=True).then_inc(s_scores, 1)

                def prob_transposes(n, slot, h):
                    if here(n):
                        if h < 2:
                            pe.wait_ge(exp_done, n * 4 + 2)
                            wait(pe, probT_act, n * 2 - 1 + h)
                        else:
                            pe.wait_ge(exp_done, n * 4 + 4)
                            pe.wait_ge(probT_dve, n * 2 + h - 1)
                        for kc in range(C):
                            for c in range(C):
                                last = pe.transpose(bank[:, PSUM_PT + h % 2, kc * T + c * P:kc * T + (c + 1) * P],
                                                    prob[:, slot, c, h, kc * P:(kc + 1) * P], ident[:])
                        last.then_inc(s_probT, 1)

                def batch_round(r, slot):
                    nxt = 1 - slot
                    if here(r + 1):
                        pe.wait_ge(y_staged[nxt], 8 * (r + 1) + (8 if nxt else 16))
                        wait(pe, qk_lo_made, r + 1)
                        wait(pe, v_made, r)
                        if here(r + LEAD - 1):
                            wait(pe, s_y, r + LEAD)
                        for c in range(C):
                            last = pe.transpose(bank[:, PSUM_QKV, c * P:(c + 1) * P], y_in[:, nxt, c, :], ident[:])
                        last.then_inc(s_yT, 1)
                    prob_transposes(r - 1, nxt, 0)
                    prob_transposes(r - 1, nxt, 1)
                    scores(r, slot, 0)
                    if here(r + 1):
                        pe.wait_ge(yT_made, r + 2)
                        for j in range(2):
                            last = pe.matmul(bank[:, PSUM_QKV, j * T:(j + 1) * T], wqkv[:, j * D:(j + 1) * D],
                                             yT[:, nxt], start=True, stop=True)
                        last.then_inc(s_qk, 1)
                    if here(r - 2):
                        pe.wait_ge(oT_made, r - 1)
                        for c in range(C):
                            last = pe.transpose(bank[:, PSUM_O, T + c * P:T + (c + 1) * P], oT[:, c * P:(c + 1) * P],
                                                ident[:])
                        last.then_inc(s_oT, 1)
                    prob_transposes(r - 1, nxt, 2)
                    prob_transposes(r - 1, nxt, 3)
                    scores(r, slot, 1)
                    scores(r, slot, 2)
                    if here(r + 1):
                        pe.wait_ge(qk_lo_made, r + 2)
                    if here(r + LEAD):
                        n = r + LEAD
                        pe.wait_ge(s_hsum, n + 1)
                        if isinstance(r, int) and r <= 0:
                            wait(pe, s_y, n)
                        for c in range(C):
                            last = pe.transpose(bank[:, PSUM_QKV, T + c * P:T + (c + 1) * P],
                                                hsum[:, nxt, c * P:(c + 1) * P], ident[:])
                        last.then_inc(s_hT, 1)
                    if here(r):
                        for c in range(C):
                            last = pe.matmul(bank[:, PSUM_QKV, c * D:(c + 1) * D], yT[:, slot, c * P:(c + 1) * P],
                                             wqkv[:, 2 * D:3 * D], start=True, stop=True)
                        last.then_inc(s_v, 1)
                    scores(r, slot, 3)
                    if here(r - 1):
                        pe.wait_ge(probT_dve, r * 2)
                        pe.wait_ge(probT_act, r * 2)
                        pe.wait_ge(v_made, r)
                        wait(pe, attn_made, r - 1)
                        for kc in range(C):
                            for h in range(HEADS):
                                rows = slice(h * HD, (h + 1) * HD)
                                last = pe.matmul(bank[rows, PSUM_O, 0:T], v[:, nxt, kc, rows], probT[:, h, kc, :],
                                                 start=(kc == 0), stop=(kc == C - 1))
                        last.then_inc(s_o, 1)

                batch_rounds(pe, batch_round)


_INS = ['x', 'adj', 'L0_gnn_Wg0', 'L0_gnn_bg0', 'L0_gnn_Wg1', 'L0_gnn_bg1', 'L0_gnn_Wih', 'L0_gnn_Whh',
        'L0_gnn_bih', 'L0_gnn_bhh', 'L1_gnn_W']
_OUTS = [((32, 256, 128), 'float32')]


def kernel(**inputs):
    import numpy as _np
    import concourse.bacc as _bacc
    from concourse import mybir as _mybir
    from concourse.bass_utils import run_bass_kernel_spmd as _run

    nc = _bacc.Bacc("TRN2", target_bir_lowering=False, num_devices=1)
    arrays, args = {}, []
    for name in _INS:
        a = _np.ascontiguousarray(inputs[name])
        arrays[f"in_{name}_dram"] = a
        args.append(nc.dram_tensor(f"in_{name}_dram", a.shape, _mybir.dt.from_np(a.dtype), kind="ExternalInput").ap())
    for i, (shape, dtype) in enumerate(_OUTS):
        dt = _mybir.dt.from_np(_np.dtype(dtype))
        args.append(nc.dram_tensor(f"out_{i}_dram", shape, dt, kind="ExternalOutput").ap())
    graph_kernel(nc, *args)
    r = _run(nc, [arrays], core_ids=[0])
    got = tuple(r.results[0][f"out_{i}_dram"] for i in range(len(_OUTS)))
    return got[0]
```
